# Optimizing a Trainium2 kernel written in Bass

```python
import numpy as np
import jax
import jax.numpy as jnp

def _softmax(x, axis=-1):
    return jax.nn.softmax(x, axis=axis)

def _gelu(x):
    return jax.nn.gelu(x, approximate=True)

def _silu(x):
    return jax.nn.silu(x)

def _sigmoid(x):
    return jax.nn.sigmoid(x)

def _layernorm(x, axis=-1, eps=1e-05):
    m = jnp.mean(x, axis=axis, keepdims=True)
    v = jnp.var(x, axis=axis, keepdims=True)
    return (x - m) / jnp.sqrt(v + eps)

def _scatter_add(tgt, idx, src, axis=0):
    return tgt.at[idx].add(src)

def _segment_sum(src, seg, n):
    return jax.ops.segment_sum(src, seg, n)
kernel_name = 'mk_adj_preln_d2_adj_r2_74ef38'

def setup_inputs(seed: int=0):
    np.random.seed(seed)
    _w = jnp.asarray

    def _rec_inputs():
        import jax
        import jax.numpy as jnp
        _gk = jax.random.key(seed)
        x = -9.806e-05 + 1 * jax.random.normal(jax.random.fold_in(_gk, 1), (8192, 64), jnp.float32)
        _w = (1.0 + jnp.arange(8192, dtype=jnp.float32)) ** (-0.5)
        _w = _w / _w.mean()
        _pij = jnp.clip(0.000244141 * _w[:, None] * _w[None, :], 0.0, 1.0)
        _a = jax.random.uniform(jax.random.fold_in(_gk, 2), (8192, 8192)) < _pij
        adj = _a.astype(jnp.int32)
        return (x, adj)
    x, adj = _rec_inputs()

    def _L0_gnn_setup():
        import jax, jax.numpy as jnp
        import numpy as np
        N = 4096
        F_IN = 64
        F_OUT = 64
        ALPHA = 0.2
        NEG_INF = -9000000000000000.0
        key = jax.random.key(seed)
        k1, k2, k3, k4 = jax.random.split(key, 4)
        h = jax.random.normal(k1, (N, F_IN), dtype=jnp.float32)
        adj = jax.random.randint(k2, (N, N), 0, 2, dtype=jnp.int32)
        W = jax.random.normal(k3, (F_OUT, F_IN), dtype=jnp.float32) * (1.0 / np.sqrt(F_IN))
        a = jax.random.normal(k4, (2 * F_OUT,), dtype=jnp.float32) * (1.0 / np.sqrt(2 * F_OUT))
        return {'h': h, 'adj': adj, 'W': W, 'a': a}
    _L0_gnn_all = _L0_gnn_setup()
    _L0_gnn_in = {k: v for k, v in _L0_gnn_all.items() if k in ('W', 'a')}
    del _L0_gnn_all

    def _L1_gnn_setup():
        import jax, jax.numpy as jnp
        import numpy as np
        ALPHA = 0.2
        NEG_INF = -9000000000000000.0
        key = jax.random.key(seed)
        k1, k2, k3, k4 = jax.random.split(key, 4)
        N, F_IN, F_OUT = (512, 64, 64)
        h = jax.random.normal(k1, (N, F_IN), dtype=jnp.float32)
        adj = jax.random.randint(k2, (N, N), 0, 2, dtype=jnp.int32)
        lim_W = 1.414 * np.sqrt(6.0 / (F_IN + F_OUT))
        W = jax.random.uniform(k3, (F_IN, F_OUT), minval=-lim_W, maxval=lim_W, dtype=jnp.float32)
        lim_a = 1.414 * np.sqrt(6.0 / (2 * F_OUT + 1))
        a = jax.random.uniform(k4, (2 * F_OUT, 1), minval=-lim_a, maxval=lim_a, dtype=jnp.float32)
        return {'h': h, 'adj': adj, 'W': W, 'a': a}
    _L1_gnn_all = _L1_gnn_setup()
    _L1_gnn_in = {k: v for k, v in _L1_gnn_all.items() if k in ('W', 'a')}
    del _L1_gnn_all
    return {'x': x, 'adj': adj, 'L0_gnn_W': _L0_gnn_in['W'], 'L0_gnn_a': _L0_gnn_in['a'], 'L1_gnn_W': _L1_gnn_in['W'], 'L1_gnn_a': _L1_gnn_in['a']}

def reference(x, adj, L0_gnn_W, L0_gnn_a, L1_gnn_W, L1_gnn_a):
    import jax
    import jax.numpy as jnp

    def _L0_gnn_ref(h, adj, W, a):
        import jax, jax.numpy as jnp
        import numpy as np
        N = 4096
        F_IN = 64
        F_OUT = 64
        ALPHA = 0.2
        NEG_INF = -9000000000000000.0
        Wh = h @ W.T
        a1, a2 = (a[:F_OUT], a[F_OUT:])
        src = Wh @ a1
        dst = Wh @ a2
        e = jax.nn.leaky_relu(src[:, None] + dst[None, :], negative_slope=ALPHA)
        scores = jnp.where(adj > 0, e, NEG_INF)
        attention = jax.nn.softmax(scores, axis=1)
        h_prime = attention @ Wh
        return jax.nn.elu(h_prime)

    def _L1_gnn_ref(h, adj, W, a):
        import jax, jax.numpy as jnp
        import numpy as np
        ALPHA = 0.2
        NEG_INF = -9000000000000000.0
        F_OUT = W.shape[1]
        Wh = h @ W
        a1, a2 = (a[:F_OUT, 0], a[F_OUT:, 0])
        e = (Wh @ a1)[:, None] + (Wh @ a2)[None, :]
        e = jax.nn.leaky_relu(e, negative_slope=ALPHA)
        scores = jnp.where(adj > 0, e, jnp.float32(NEG_INF))
        attention = jax.nn.softmax(scores, axis=1)
        h_prime = attention @ Wh
        return jax.nn.elu(h_prime)
    h = jnp.maximum(_layernorm(x, axis=-1), 0.0)
    x = x + _L0_gnn_ref(h, adj, L0_gnn_W, L0_gnn_a)
    h = jnp.maximum(_layernorm(x, axis=-1), 0.0)
    x = x + _L1_gnn_ref(h, adj, L1_gnn_W, L1_gnn_a)
    return x

_drawn_inputs = setup_inputs


def setup_inputs(seed=0):
    import zlib

    import numpy as np

    out = dict(_drawn_inputs(seed))
    spreads = {}
    factors = {}
    for name, (base, spread) in spreads.items():
        noise = np.random.default_rng([zlib.crc32(name.encode()), seed]).standard_normal(out[name].shape)
        drawn = base * np.exp(spread * noise) if base else spread * noise
        out[name] = jnp.asarray(drawn.astype(out[name].dtype))
    for name, factor in factors.items():
        out[name] = (out[name] * factor).astype(out[name].dtype)
    return out
```

```python
from contextlib import ExitStack

import concourse.bass as bass
from concourse import mybir

F32, I32, U32, BF16 = mybir.dt.float32, mybir.dt.int32, mybir.dt.uint32, mybir.dt.bfloat16
ALU, ACT, AX = mybir.AluOpType, mybir.ActivationFunctionType, mybir.AxisListType

P = 128
N = 8192
F = 64
TILES = N // P
SPARSE = TILES - 1
ROW = F + 2
SCORE_COL, OWN_COL = F, F + 1
MEAN_ROW = N
SKIP = 1 << 20
SLOTS = 16
ALWAYS = 4
STEPS = (4, 5, 6, 7, 8, 10, 12, 16)
SEGS = (0, 512, 2048, 4608, 8192)
NSEG = len(SEGS) - 1
FOUND = 8 * NSEG
G4 = 4
GROUPS = TILES // G4
ALPHA, NEG, EPS = 0.2, -9000000000000000.0, 1e-5


def build(nc, x, adj, w0, a0, w1, a1, out):
    tabs = [nc.dram_tensor(f"table{l}", (N + 1, ROW), F32, kind="Internal").ap() for l in range(2)]
    scores_row = [nc.dram_tensor(f"scores{l}", (N,), F32, kind="Internal").ap() for l in range(2)]
    wh_cols = [nc.dram_tensor(f"wh_columns{l}", (F, N), F32, kind="Internal").ap() for l in range(2)]

    with ExitStack() as ctx:
        def sb(name, shape, dt=F32):
            return ctx.enter_context(nc.sbuf_tensor(name, shape, dt))

        def sem(name):
            return ctx.enter_context(nc.semaphore(name))

        ring = [sb(f"ring{b}", [P, N], I32) for b in range(2)]
        ringf = [r[:, :].bitcast(F32) for r in ring]
        both_signs = sb("both_signs", [P, 2 * (N + FOUND)], BF16)
        signs = [both_signs[:, b * (N + FOUND):(b + 1) * (N + FOUND)] for b in range(2)]
        feature = both_signs[:, 0:2 * N].bitcast(F32)
        xs = sb("xs", [P, TILES * F])
        acc = sb("acc", [P, TILES * F])
        wh = sb("wh", [P, TILES * ROW])
        G = [sb(f"G{b}", [P, SLOTS * ROW]) for b in range(2)]
        prod = [sb(f"prod{b}", [P, SLOTS * F]) for b in range(2)]
        lists = sb("lists", [P, SPARSE * SLOTS], U32)
        slot_idx = [sb(f"slot_idx{b}", [P, SLOTS], U32) for b in range(2)]
        hst = [sb(f"hst{b}", [P, G4 * F]) for b in range(2)]
        hT = [sb(f"hT{b}", [F, G4 * P]) for b in range(2)]
        pT = [sb(f"pT{b}", [P, G4 * P]) for b in range(2)]
        ident = sb("ident", [P, P])
        ones8 = sb("ones8", [P, 8], BF16)
        over_n = sb("over_n", [P, 1])
        seg_base = sb("seg_base", [P, FOUND])
        seg_len = sb("seg_len", [P, FOUND])
        none_at = sb("none_at", [P, SLOTS])
        found = [sb(f"found{b}", [P, FOUND], U32) for b in range(2)]
        key0 = sb("key0", [P, FOUND])
        valid = sb("valid", [P, FOUND])
        key = sb("key", [P, FOUND])
        top = sb("top", [P, SLOTS])
        gap = sb("gap", [P, SLOTS])
        degree = [sb(f"degree{b}", [P, 1]) for b in range(2)]
        degree_max = sb("degree_max", [P, 1])
        last_key = sb("last_key", [P, 1])
        seg_over = sb("seg_over", [P, 1])
        over = sb("over", [P, 1])
        counts = sb("counts", [1, SPARSE], I32)
        flag = sb("flag", [1, 1], I32)
        z = sb("z", [P, SLOTS])
        e = [sb(f"e{b}", [P, SLOTS]) for b in range(2)]
        pen = sb("pen", [P, SLOTS])
        rowmax = sb("rowmax", [P, 1])
        negmax = [sb(f"negmax{b}", [P, 1]) for b in range(2)]
        pexp = [sb(f"pexp{b}", [P, SLOTS]) for b in range(2)]
        pw = sb("pw", [P, SLOTS])
        sums = sb("sums", [P, TILES])
        rsums = sb("rsums", [P, TILES])
        mean = sb("mean", [P, TILES])
        var = sb("var", [P, TILES])
        std = sb("std", [P, TILES])
        rstd = sb("rstd", [P, TILES])
        mean_wh = sb("mean_wh", [1, ROW])
        scores_t = sb("scores_t", [TILES, P])
        dense_max = sb("dense_max", [P, 1])
        dense_neg = sb("dense_neg", [P, 1])
        w_in = [sb(f"w_in{l}", [F, F]) for l in range(2)]
        a_in = [sb(f"a_in{l}", [F, 2]) for l in range(2)]
        w_t = [sb(f"w_t{l}", [F, F]) for l in range(2)]
        wx = [sb(f"wx{l}", [F, ROW]) for l in range(2)]

        def ps(name):
            return ctx.enter_context(nc.psum_tensor(name, [P, 512], F32))

        psT = [ps(f"psT{b}") for b in range(2)]
        psW = [ps(f"psW{b}") for b in range(2)]
        psS = [ps(f"psS{b}") for b in range(2)]
        psD = [ps(f"psD{b}") for b in range(2)]

        x_landed = sem("x_landed")
        w_landed = sem("w_landed")
        consts = sem("consts")
        consts0 = sem("consts0")
        zeroed = sem("zeroed")
        sentinels_set = sem("sentinels_set")
        passed = [sem(f"passed_{name}") for name in ("pe", "pool", "dve")]
        w_turned = sem("w_turned")
        wt_copied = sem("wt_copied")
        a_through = sem("a_through")
        wx_ready = sem("wx_ready")
        var_ready = sem("var_ready")
        std_ready = sem("std_ready")
        h_ready = sem("h_ready")
        h_turned = sem("h_turned")
        hT_ready = sem("hT_ready")
        wh_done = sem("wh_done")
        wh_copied = sem("wh_copied")
        mean_summed = sem("mean_summed")
        mean_ready = sem("mean_ready")
        table_stored = sem("table_stored")
        dense_landed = sem("dense_landed")
        dense_scored = sem("dense_scored")
        dense_exped = sem("dense_exped")
        p_turned = sem("p_turned")
        pT_ready = sem("pT_ready")
        dense_block = sem("dense_block")
        dense_copied = sem("dense_copied")
        adj_landed = [sem(f"adj_landed{b}") for b in range(2)]
        signed = sem("signed")
        searched = sem("searched")
        listed = sem("listed")
        degrees_turned = sem("degrees_turned")
        counted = sem("counted")
        idx_copied = sem("idx_copied")
        neighbours_in = sem("neighbours_in")
        gathered = [sem(f"gathered{b}") for b in range(2)]
        scored = sem("scored")
        exped = sem("exped")
        weighted = sem("weighted")
        summed = sem("summed")
        acc_copied = sem("acc_copied")
        over_ready = sem("over_ready")
        over_turned = sem("over_turned")
        flag_ready = sem("flag_ready")
        neg_ready = sem("neg_ready")
        elu_exped = sem("elu_exped")
        y_ready = sem("y_ready")
        out_stored = sem("out_stored")
        g_column = [sem(f"g_column{l}") for l in range(2)]
        g_landed = [sem(f"g_landed{l}") for l in range(2)]
        g_scored = [sem(f"g_scored{l}") for l in range(2)]
        g_exped = [sem(f"g_exped{l}") for l in range(2)]
        g_feature = [sem(f"g_feature{l}") for l in range(2)]
        g_used = [sem(f"g_used{l}") for l in range(2)]

        def past(n, least):
            return not isinstance(n, int) or n >= least

        def stand_alone(eng, which):
            eng.sem_inc(passed[which], 1)

        def tile_rows(t):
            return bass.ds(t * P, P) if not isinstance(t, int) else slice(t * P, (t + 1) * P)

        def cols(t, w):
            return bass.ds(t * w, w) if not isinstance(t, int) else slice(t * w, (t + 1) * w)

        def sparse_tiles(eng, body, peel):
            for n in range(peel):
                body(n, n // 2, n % 2)
            with eng.Fori(peel // 2, SPARSE // 2) as i:
                for b in range(2):
                    body(i * 2 + b, i, b)
            body(SPARSE - 1, SPARSE // 2, 0)

        def groups(eng, body):
            for g in range(2):
                body(g, g)
            with eng.Fori(1, GROUPS // 2) as i:
                for b in range(2):
                    body(i * 2 + b, b)

        block = ctx.enter_context(nc.Block())

        @block.sync
        def _(sp):
            sp.dma_start(w_in[0][:, :], w0).then_inc(w_landed, 16)
            sp.dma_start(w_in[1][:, :], w1).then_inc(w_landed, 16)
            for l, a in enumerate((a0, a1)):
                sp.dma_start(a_in[l][:, 0:1], a[F:2 * F, :]).then_inc(w_landed, 16)
                sp.dma_start(a_in[l][:, 1:2], a[0:F, :]).then_inc(w_landed, 16)
            sp.dma_start(xs[:, :].rearrange("p (t f) -> p t f", f=F),
                         x.rearrange("(t p) f -> p t f", p=P)).then_inc(x_landed, 16)

            def store_table(l):
                sp.wait_ge(wh_copied, GROUPS * (l + 1))
                whv = wh[:, :].rearrange("p (t c) -> p t c", c=ROW)
                sp.dma_start(tabs[l][0:N, :].rearrange("(t p) c -> p t c", p=P), whv).then_inc(table_stored, 16)
                sp.wait_ge(mean_ready, l + 1)
                sp.dma_start(scores_row[l].rearrange("(t p) -> t p", p=P), scores_t[:, :]).then_inc(table_stored, 16)
                sp.dma_start(tabs[l][N:N + 1, :], mean_wh[:, :]).then_inc(table_stored, 16)
                sp.wait_ge(table_stored, 48 * (l + 1))
                sp.dma_start(ringf[1], scores_row[l].rearrange("(a n) -> a n", a=1).broadcast_to([P, N]))\
                    .then_inc(dense_landed, 16)

            sp.dma_start(ring[0][:, :], adj[0:P, :]).then_inc(dense_landed, 16)
            store_table(0)
            sp.wait_ge(dense_block, GROUPS)

            def load(n, i, b):
                if past(n, 2):
                    sp.wait_ge(signed, n - 1)
                sp.dma_start(ring[b][:, :], adj[tile_rows(n + 1), :]).then_inc(adj_landed[b], 16)

            sparse_tiles(sp, load, 2)
            sp.wait_ge(y_ready, 1)
            sp.dma_start(ring[0][:, :], adj[0:P, :]).then_inc(dense_landed, 16)
            store_table(1)
            sp.wait_ge(y_ready, 2)
            sp.dma_start(out.rearrange("(t p) f -> p t f", p=P),
                         xs[:, :].rearrange("p (t f) -> p t f", f=F)).then_inc(out_stored, 16)
            sp.wait_ge(out_stored, 16)

        @block.gpsimd
        def _(pool):
            pool.memset(ident[:, :], 0.0).then_inc(consts0, 1)
            pool.wait_ge(consts0, 1)
            pool.affine_select(out=ident[:, :], in_=ident[:, :], compare_op=ALU.not_equal, fill=1.0,
                               base=0, pattern=[[-1, P]], channel_multiplier=1).then_inc(consts, 1)
            for b in range(2):
                pool.memset(G[b][:, :], 0.0).then_inc(zeroed, 1)
            reg = pool.alloc_register("most_edges")
            landing = [pool.alloc_register(f"landing{b}") for b in range(2)]
            for b in range(2):
                pool.reg_mov(landing[b], 0)

            def gather(l, n, i, b):
                tile = SPARSE * l + n
                if l == 0:
                    pool.wait_ge(counted, n + 1)
                if past(tile, 2):
                    pool.wait_ge(weighted, tile - 1)
                pool.tensor_copy(slot_idx[b][:, :], lists[:, cols(n, SLOTS)]).then_inc(idx_copied, 1)
                pool.reg_load(reg, counts[0:1, bass.ds(n, 1)] if not isinstance(n, int) else counts[0:1, n:n + 1])
                most = pool.snap(reg, min_val=0, max_val=FOUND)
                pool.wait_ge(idx_copied, tile + 1)
                stand_alone(pool, 1)

                def slots(first, last):
                    for k in range(first, last):
                        pool.indirect_dma_start(
                            out=G[b][:, k * ROW:(k + 1) * ROW], out_offset=None, in_=tabs[l],
                            in_offset=bass.IndirectOffsetOnAxis(ap=slot_idx[b][:, k:k + 1], axis=0),
                            bounds_check=MEAN_ROW, oob_is_err=False).then_inc(gathered[b], 16)

                slots(0, ALWAYS)
                pool.reg_add(landing[b], landing[b], 16 * ALWAYS)
                if l == 1 and not (isinstance(n, int) and n < 1):
                    all_in(1 - b)
                for first, last in zip(STEPS, STEPS[1:]):
                    with pool.If(most > first):
                        slots(first, last)
                        pool.reg_add(landing[b], landing[b], 16 * (last - first))
                    with pool.Else():
                        pool.nop()
                if l == 0:
                    all_in(b)

            def all_in(b):
                pool.wait_ge(gathered[b], pool.snap(landing[b], min_val=0, max_val=1 << 15))
                pool.sem_inc(neighbours_in, 1)

            for l in range(2):
                pool.wait_ge(table_stored, 48 * (l + 1))
                sparse_tiles(pool, lambda n, i, b: gather(l, n, i, b), 2)
            all_in(0)

        @block.scalar
        def _(act):
            act.wait_ge(w_turned, 2)
            for l in range(2):
                act.activation(w_t[l][:, :], psT[l][0:F, 0:F], ACT.Copy).then_inc(wt_copied, 1)
            act.wait_ge(a_through, 2)
            act.wait_ge(wt_copied, 2)
            act.activation(wx[0][:, 0:F], w_t[0][:, :], ACT.Copy).then_inc(wx_ready, 1)
            act.wait_ge(w_landed, 96)
            act.activation(wx[1][:, 0:F], w_in[1][:, :], ACT.Copy).then_inc(wx_ready, 1)
            for l in range(2):
                act.activation(wx[l][:, F:ROW], psW[l][0:F, 0:2], ACT.Copy).then_inc(wx_ready, 1)

            def features(l):
                act.wait_ge(var_ready, l + 1)
                act.activation(std[:, :], var[:, :], ACT.Sqrt).then_inc(std_ready, 1)

                def group(g, b):
                    at = GROUPS * l + g
                    act.wait_ge(h_turned, at + 1)
                    if past(at, 2):
                        act.wait_ge(wh_done, at - 1)
                    act.activation(hT[b][:, :], psT[b][0:F, :], ACT.Copy).then_inc(hT_ready, 1)
                    act.wait_ge(wh_done, at + 1)
                    act.activation(wh[:, cols(g, G4 * ROW)], psW[b][:, 0:G4 * ROW], ACT.Copy).then_inc(wh_copied, 1)

                groups(act, group)

            def dense(l):
                act.wait_ge(dense_scored, l + 1)
                act.activation(ringf[1], ringf[1], ACT.Exp, bias=dense_neg[:, :],
                               accum_out=sums[:, 0:1]).then_inc(dense_exped, 1)
                for q in range(GROUPS):
                    at = GROUPS * l + q
                    act.wait_ge(p_turned, at + 1)
                    if past(at, 2):
                        act.wait_ge(dense_block, at - 1)
                    act.activation(pT[q % 2][:, :], psT[q % 2][:, :], ACT.Copy).then_inc(pT_ready, 1)
                act.wait_ge(dense_block, GROUPS * (l + 1))
                act.activation(acc[:, 0:F], psS[0][:, 0:F], ACT.Copy).then_inc(dense_copied, 1)

            def exp(l, n, b):
                act.wait_ge(scored, SPARSE * l + n + 1)
                act.activation(pexp[b][:, :], e[b][:, :], ACT.Exp, bias=negmax[b][:, :]).then_inc(exped, 1)

            def copy_sum(l, n, b):
                act.wait_ge(summed, SPARSE * l + n + 1)
                act.activation(acc[:, cols(n + 1, F)], psS[b][:, 0:F], ACT.Copy).then_inc(acc_copied, 1)

            def sign(n, i, b):
                act.wait_ge(adj_landed[b], (i + 1) * 16)
                if past(n, 2):
                    act.wait_ge(searched, n - 1)
                for s in range(NSEG):
                    lo, hi = SEGS[s], SEGS[s + 1]
                    done = act.activation(signs[b][:, lo + 8 * s:hi + 8 * s], ring[b][:, lo:hi], ACT.Sign)
                    if s == 0 and not (isinstance(n, int) and n < 3):
                        exp(0, n - 3, 1 - b)
                done.then_inc(signed, 1)
                if not (isinstance(n, int) and n < 4):
                    copy_sum(0, n - 4, b)

            def general(l):
                reg = act.alloc_register(f"act_flag{l}")
                act.wait_ge(flag_ready, 1)
                act.wait_ge(g_used[l], 1)
                act.reg_load(reg, flag[0:1, 0:1])
                some = act.snap(reg, min_val=0, max_val=N)
                with act.If(some > 0):
                    with act.Fori(0, F) as f:
                        act.dma_start(wh_cols[l][bass.ds(f, 1), :],
                                      tabs[l][0:N, bass.ds(f, 1)].rearrange("n a -> a n"),
                                      allow_slow_non_contiguous=True).then_inc(g_column[l], 16)
                        act.wait_ge(g_column[l], f * 16 + 16)
                    with act.Fori(0, TILES) as t:
                        act.wait_ge(g_used[l], t * (F + 1) + 1)
                        act.dma_start(ring[0][:, :], adj[bass.ds(t * P, P), :]).then_inc(g_landed[l], 16)
                        act.dma_start(ringf[1], scores_row[l].rearrange("(a n) -> a n", a=1).broadcast_to([P, N]))\
                            .then_inc(g_landed[l], 16)
                        act.wait_ge(g_scored[l], t + 1)
                        act.activation(ringf[1], ringf[1], ACT.Exp, bias=dense_neg[:, :],
                                       accum_out=dense_max[:, :]).then_inc(g_exped[l], 1)
                        with act.Fori(0, F) as f:
                            act.wait_ge(g_used[l], t * (F + 1) + f + 1)
                            act.dma_start(feature[:, :], wh_cols[l][bass.ds(f, 1), :].broadcast_to([P, N]))\
                                .then_inc(g_feature[l], 16)
                with act.Else():
                    act.nop()

            def elu(l):
                act.wait_ge(neg_ready, l + 1)
                act.activation(ringf[0][:, 0:TILES * F], ringf[0][:, 0:TILES * F], ACT.Exp).then_inc(elu_exped, 1)

            features(0)
            dense(0)
            act.wait_ge(sentinels_set, 1)
            sparse_tiles(act, sign, 4)
            for n in range(SPARSE - 3, SPARSE):
                exp(0, n, n % 2)
                copy_sum(0, n - 1, (n - 1) % 2)
            copy_sum(0, SPARSE - 1, 0)
            general(0)
            elu(0)
            features(1)
            dense(1)

            def second(n, i, b):
                exp(1, n, b)
                copy_sum(1, n, b)

            sparse_tiles(act, second, 2)
            general(1)
            elu(1)

        @block.tensor
        def _(pe):
            pe.wait_ge(consts, 1)
            pe.wait_ge(sentinels_set, 1)
            pe.wait_ge(w_landed, 96)
            for l in range(2):
                pe.transpose(psT[l][0:F, 0:F], w_in[l][:, :], ident[0:F, 0:F]).then_inc(w_turned, 1)
            pe.matmul(psW[0][0:F, 0:2], w_in[0][:, :], a_in[0][:, :], start=True, stop=True).then_inc(a_through, 1)
            pe.wait_ge(wt_copied, 2)
            pe.matmul(psW[1][0:F, 0:2], w_t[1][:, :], a_in[1][:, :], start=True, stop=True).then_inc(a_through, 1)
            pe.wait_ge(wx_ready, 4)

            def features(l):
                def group(g, b):
                    at = GROUPS * l + g
                    pe.wait_ge(h_ready, at + 1)
                    if past(at, 2):
                        pe.wait_ge(hT_ready, at - 1)
                    stand_alone(pe, 0)
                    for k in range(G4):
                        done = pe.transpose(psT[b][0:F, k * P:(k + 1) * P], hst[b][:, k * F:(k + 1) * F], ident[:, :])
                    done.then_inc(h_turned, 1)
                    pe.wait_ge(hT_ready, at + 1)
                    if past(at, 2):
                        pe.wait_ge(wh_copied, at - 1)
                    for k in range(G4):
                        done = pe.matmul(psW[b][:, k * ROW:(k + 1) * ROW], hT[b][:, k * P:(k + 1) * P],
                                         wx[l][:, :], start=True, stop=True)
                    done.then_inc(wh_done, 1)

                groups(pe, group)
                pe.wait_ge(wh_copied, GROUPS * (l + 1))
                for q in range(GROUPS):
                    done = pe.matmul(psD[1][0:1, 0:G4 * ROW], over_n[:, :], wh[:, q * G4 * ROW:(q + 1) * G4 * ROW],
                                     start=(q == 0), stop=(q == GROUPS - 1))
                if l:
                    pe.wait_ge(flag_ready, l)
                scores = wh[:, :].rearrange("p (t c) -> p t c", c=ROW)[:, :, SCORE_COL]
                done = pe.matmul(psD[0][0:TILES, 0:P], scores, ident[:, :], start=True, stop=True)
                done.then_inc(mean_summed, 1)

            def dense(l):
                pe.wait_ge(dense_exped, l + 1)
                pe.wait_ge(wh_copied, GROUPS * (l + 1))
                if l:
                    pe.wait_ge(acc_copied, SPARSE * l)
                for q in range(GROUPS + 1):
                    if q < GROUPS:
                        if past(GROUPS * l + q, 2):
                            pe.wait_ge(pT_ready, GROUPS * l + q - 1)
                        for k in range(G4):
                            j = q * G4 + k
                            done = pe.transpose(psT[q % 2][:, k * P:(k + 1) * P], ringf[1][:, j * P:(j + 1) * P], ident[:, :])
                        done.then_inc(p_turned, 1)
                    if q > 0:
                        pe.wait_ge(pT_ready, GROUPS * l + q)
                        for k in range(G4):
                            j = (q - 1) * G4 + k
                            done = pe.matmul(psS[0][:, 0:F], pT[(q - 1) % 2][:, k * P:(k + 1) * P],
                                             wh[:, j * ROW:j * ROW + F], start=(j == 0), stop=(j == TILES - 1))
                        done.then_inc(dense_block, 1)
                pe.wait_ge(dense_copied, l + 1)

            def turn_degrees(n, b):
                pe.wait_ge(listed, n + 1)
                if past(n, 2):
                    pe.wait_ge(counted, n - 1)
                pe.matmul(psD[b][0:1, 0:P], degree[b][:, :], ident[:, :], start=True, stop=True).then_inc(degrees_turned, 1)

            def sum_slots(l, n, b):
                pe.wait_ge(weighted, SPARSE * l + n + 1)
                if past(SPARSE * l + n, 2):
                    pe.wait_ge(acc_copied, SPARSE * l + n - 1)
                for k in range(SLOTS):
                    done = pe.matmul(psS[b][:, 0:F], ident[:, :], prod[b][:, k * F:(k + 1) * F],
                                     start=(k == 0), stop=(k == SLOTS - 1))
                done.then_inc(summed, 1)

            def first(n, i, b):
                if not (isinstance(n, int) and n < 2):
                    sum_slots(0, n - 2, b)
                turn_degrees(n, b)

            features(0)
            dense(0)
            pe.wait_ge(mean_ready, 1)
            sparse_tiles(pe, first, 4)
            for n in (SPARSE - 2, SPARSE - 1):
                sum_slots(0, n, n % 2)
            pe.wait_ge(over_ready, 1)
            pe.matmul(psD[0][0:1, 0:P], over[:, :], ident[:, :], start=True, stop=True).then_inc(over_turned, 1)
            features(1)
            dense(1)
            sparse_tiles(pe, lambda n, i, b: sum_slots(1, n, b), 2)

        @block.vector
        def _(dve):
            dve.memset(ones8[:, :], 1.0)
            dve.memset(over_n[:, :], 1.0 / N)
            for s in range(NSEG):
                dve.memset(seg_base[:, 8 * s:8 * s + 8], float(SEGS[s] + 1))
                dve.memset(seg_len[:, 8 * s:8 * s + 8], float(SEGS[s + 1] - SEGS[s]))
                for b in range(2):
                    end = SEGS[s + 1] + 8 * s
                    dve.memset(signs[b][:, end:end + 8], 1.0)
            dve.memset(none_at[:, 0:1], float(MEAN_ROW + 1))
            dve.memset(none_at[:, 1:SLOTS], float(SKIP))
            dve.memset(degree_max[:, :], 0.0)
            dve.memset(seg_over[:, :], 0.0)
            dve.drain()
            dve.memset(pw[:, :], 0.0).then_inc(sentinels_set, 1)

            xv = xs[:, :].rearrange("p (t f) -> p t f", f=F)
            av = acc[:, :].rearrange("p (t f) -> p t f", f=F)
            whv = wh[:, :].rearrange("p (t c) -> p t c", c=ROW)
            sq = ringf[1][:, 0:TILES * F]
            sqv = sq.rearrange("p (t f) -> p t f", f=F)
            mnv = ringf[0][:, 0:TILES * F]

            def over_features(v):
                return v[:, :].rearrange("p (t a) -> p t a", a=1).broadcast_to([P, TILES, F])

            def features(l):
                if l == 0:
                    dve.wait_ge(x_landed, 16)
                dve.tensor_reduce(mean[:, :], xv, AX.X, ALU.add)
                dve.drain()
                dve.tensor_scalar(mean[:, :], mean[:, :], 1.0 / F, None, ALU.mult)
                dve.drain()
                dve.tensor_tensor(av, xv, over_features(mean), ALU.subtract)
                dve.drain()
                dve.tensor_tensor(sq, acc[:, :], acc[:, :], ALU.mult)
                dve.drain()
                dve.tensor_reduce(var[:, :], sqv, AX.X, ALU.add)
                dve.drain()
                dve.tensor_scalar(var[:, :], var[:, :], 1.0 / F, EPS, ALU.mult, ALU.add).then_inc(var_ready, 1)
                dve.wait_ge(std_ready, l + 1)
                dve.reciprocal(rstd[:, :], std[:, :])
                dve.drain()

                def group(g, b):
                    if past(GROUPS * l + g, 2):
                        dve.wait_ge(h_turned, GROUPS * l + g - 1)
                    r = rstd[:, cols(g, G4)].rearrange("p (t a) -> p t a", a=1).broadcast_to([P, G4, F])
                    dve.scalar_tensor_tensor(hst[b][:, :].rearrange("p (t f) -> p t f", f=F),
                                             acc[:, cols(g, G4 * F)].rearrange("p (t f) -> p t f", f=F),
                                             0.0, r, ALU.max, ALU.mult).then_inc(h_ready, 1)

                groups(dve, group)
                dve.wait_ge(mean_summed, l + 1)
                dve.tensor_copy(scores_t[:, :], psD[0][0:TILES, 0:P])
                dve.drain()
                dve.tensor_reduce(mean_wh[:, :], psD[1][0:1, 0:G4 * ROW].rearrange("p (k c) -> p c k", c=ROW),
                                  AX.X, ALU.add).then_inc(mean_ready, 1)

            def dense_scores(own):
                e1, m = ringf[1], ringf[0]
                dve.tensor_scalar(m, ring[0][:, :], 0, None, ALU.is_gt)
                dve.tensor_scalar(e1, e1, own, None, ALU.add)
                dve.drain()
                dve.scalar_tensor_tensor(e1, e1, ALPHA, e1, ALU.mult, ALU.max)
                dve.drain()
                dve.tensor_tensor(e1, e1, m, ALU.mult)
                dve.drain()
                dve.tensor_scalar(m, m, 1.0, -NEG, ALU.subtract, ALU.mult)
                dve.drain()
                dve.tensor_tensor(e1, e1, m, ALU.add)
                dve.drain()
                dve.tensor_reduce(dense_max[:, :], e1, AX.X, ALU.max)
                dve.drain()
                return dve.tensor_scalar(dense_neg[:, :], dense_max[:, :], -1.0, None, ALU.mult)

            def dense(l):
                dve.wait_ge(dense_landed, 32 * (l + 1))
                dense_scores(whv[:, 0, OWN_COL:ROW]).then_inc(dense_scored, 1)

            def search(n, b, first, last):
                for s in range(first, last):
                    done = dve.max_index(found[b][:, 8 * s:8 * s + 8], ones8[:, :],
                                         signs[b][:, SEGS[s] + 8 * s:SEGS[s + 1] + 8 * s + 8])
                if last == NSEG:
                    done.then_inc(searched, 1)

            def make_list(n, b):
                dve.drain()
                dve.tensor_tensor(key0[:, :], found[b][:, :], seg_base[:, :], ALU.add)
                dve.scalar_tensor_tensor(valid[:, :], found[b][:, :], 1.0, seg_len[:, :], ALU.mult, ALU.is_lt,
                                         accum_out=degree[b][:, :])
                dve.drain()
                dve.tensor_tensor(key[:, :], key0[:, :], valid[:, :], ALU.mult)
                dve.tensor_tensor(degree_max[:, :], degree_max[:, :], degree[b][:, :], ALU.max)
                dve.drain()
                dve.max(top[:, 0:8], key[:, :])
                dve.tensor_reduce(last_key[:, :], valid[:, 7:FOUND:8], AX.X, ALU.max)
                dve.drain()
                dve.match_replace(key0[:, :], top[:, 0:8], key[:, :], 0.0)
                dve.tensor_tensor(seg_over[:, :], seg_over[:, :], last_key[:, :], ALU.max)
                dve.drain()
                dve.max(top[:, 8:16], key0[:, :])
                dve.drain()
                dve.scalar_tensor_tensor(gap[:, :], top[:, :], 0.0, none_at[:, :], ALU.is_equal, ALU.mult)
                dve.drain()
                dve.scalar_tensor_tensor(lists[:, cols(n, SLOTS)], top[:, :], -1.0, gap[:, :], ALU.add, ALU.add)\
                    .then_inc(listed, 1)

            def count(n, b):
                dve.wait_ge(degrees_turned, n + 1)
                dve.tensor_reduce(counts[0:1, bass.ds(n, 1)] if not isinstance(n, int) else counts[0:1, n:n + 1],
                                  psD[b][0:1, 0:P], AX.X, ALU.max).then_inc(counted, 1)

            def score(l, n, i, b):
                dve.wait_ge(neighbours_in, SPARSE * l + n + 1)
                dcol = G[b][:, :].rearrange("p (k c) -> p k c", c=ROW)[:, :, SCORE_COL]
                own = wh[:, bass.ds((n + 1) * ROW + OWN_COL, 1)] if not isinstance(n, int) else \
                    wh[:, (n + 1) * ROW + OWN_COL:(n + 2) * ROW]
                dve.tensor_scalar(z[:, :], dcol, own, None, ALU.add)
                dve.tensor_scalar(pen[:, :], slot_idx[b][:, :], float(MEAN_ROW), NEG, ALU.is_gt, ALU.mult)
                dve.drain()
                dve.scalar_tensor_tensor(z[:, :], z[:, :], ALPHA, z[:, :], ALU.mult, ALU.max)
                dve.drain()
                dve.tensor_tensor(e[b][:, :], z[:, :], pen[:, :], ALU.add)
                dve.drain()
                dve.tensor_reduce(rowmax[:, :], e[b][:, :], AX.X, ALU.max)
                dve.drain()
                dve.tensor_scalar(negmax[b][:, :], rowmax[:, :], -1.0, None, ALU.mult).then_inc(scored, 1)

            def weigh(l, n, b):
                dve.wait_ge(exped, SPARSE * l + n + 1)
                total = sums[:, bass.ds(n + 1, 1)] if not isinstance(n, int) else sums[:, n + 1:n + 2]
                dve.scalar_tensor_tensor(pw[:, :], slot_idx[b][:, :], float(MEAN_ROW), pexp[b][:, :],
                                         ALU.is_le, ALU.mult, accum_out=total)
                dve.drain()
                if past(SPARSE * l + n, 2):
                    dve.wait_ge(summed, SPARSE * l + n - 1)
                dve.tensor_tensor(prod[b][:, :].rearrange("p (k f) -> p k f", f=F),
                                  G[b][:, :].rearrange("p (k c) -> p k c", c=ROW)[:, :, 0:F],
                                  pw[:, :].rearrange("p (k a) -> p k a", a=1).broadcast_to([P, SLOTS, F]),
                                  ALU.mult).then_inc(weighted, 1)

            def stream(n, i, b):
                dve.wait_ge(signed, n + 1)
                stand_alone(dve, 2)
                search(n, b, 0, 2)
                if not (isinstance(n, int) and n < 2):
                    weigh(0, n - 2, b)
                search(n, b, 2, NSEG)
                make_list(n, b)
                if not (isinstance(n, int) and n < 1):
                    score(0, n - 1, i + b - 1, 1 - b)
                count(n, b)

            def general(l):
                reg = dve.alloc_register(f"dve_flag{l}")
                dve.wait_ge(flag_ready, 1)
                dve.drain()
                dve.reg_load(reg, flag[0:1, 0:1])
                some = dve.snap(reg, min_val=0, max_val=N)
                dve.drain().then_inc(g_used[l], 1)
                with dve.If(some > 0):
                    with dve.Fori(0, TILES) as t:
                        dve.wait_ge(g_landed[l], t * 32 + 32)
                        dense_scores(wh[:, bass.ds(t * ROW + OWN_COL, 1)]).then_inc(g_scored[l], 1)
                        dve.wait_ge(g_exped[l], t + 1)
                        dve.tensor_copy(sums[:, bass.ds(t, 1)], dense_max[:, :])
                        with dve.Fori(0, F) as f:
                            dve.wait_ge(g_feature[l], (t * F + f) * 16 + 16)
                            dve.scalar_tensor_tensor(ringf[0], ringf[1], 1.0, feature[:, :], ALU.mult, ALU.mult,
                                                     accum_out=acc[:, bass.ds(t * F + f, 1)]).then_inc(g_used[l], 1)
                            dve.drain()
                        dve.drain().then_inc(g_used[l], 1)
                with dve.Else():
                    dve.nop()
                dve.drain()

            def residual(l):
                dve.reciprocal(rsums[:, :], sums[:, :])
                dve.drain()
                dve.tensor_tensor(av, av, over_features(rsums), ALU.mult)
                dve.drain()
                dve.tensor_scalar(mnv, acc[:, :], 0.0, None, ALU.min).then_inc(neg_ready, 1)
                dve.tensor_scalar(acc[:, :], acc[:, :], 0.0, None, ALU.max)
                dve.wait_ge(elu_exped, l + 1)
                dve.drain()
                dve.scalar_tensor_tensor(acc[:, :], mnv, -1.0, acc[:, :], ALU.add, ALU.add)
                dve.drain()
                dve.tensor_tensor(xs[:, :], xs[:, :], acc[:, :], ALU.add).then_inc(y_ready, 1)
                dve.drain()

            features(0)
            dense(0)
            sparse_tiles(dve, stream, 4)
            weigh(0, SPARSE - 2, 1)
            score(0, SPARSE - 1, SPARSE // 2, 0)
            weigh(0, SPARSE - 1, 0)
            dve.scalar_tensor_tensor(over[:, :], degree_max[:, :], float(-SLOTS), seg_over[:, :], ALU.add, ALU.max)\
                .then_inc(over_ready, 1)
            dve.wait_ge(over_turned, 1)
            dve.tensor_reduce(flag[:, :], psD[0][0:1, 0:P], AX.X, ALU.max).then_inc(flag_ready, 1)
            dve.wait_ge(acc_copied, SPARSE)
            dve.wait_ge(dense_copied, 1)
            general(0)
            residual(0)
            features(1)
            dense(1)

            def second(n, i, b):
                score(1, n, i, b)
                weigh(1, n, b)

            sparse_tiles(dve, second, 2)
            dve.wait_ge(acc_copied, 2 * SPARSE)
            dve.wait_ge(dense_copied, 2)
            general(1)
            residual(1)


def kernel(**inputs):
    import numpy as np
    import concourse.bacc as bacc
    from concourse.bass_utils import run_bass_kernel_spmd as run

    names = ("x", "adj", "L0_gnn_W", "L0_gnn_a", "L1_gnn_W", "L1_gnn_a")
    nc = bacc.Bacc("TRN2", target_bir_lowering=False, num_devices=1)
    arrays, args = {}, []
    for name in names:
        a = np.ascontiguousarray(inputs[name])
        if name.endswith("_a"):
            a = a.reshape(2 * F, 1)
        arrays[f"in_{name}"] = a
        args.append(nc.dram_tensor(f"in_{name}", a.shape, mybir.dt.from_np(a.dtype), kind="ExternalInput").ap())
    y = nc.dram_tensor("y", (N, F), F32, kind="ExternalOutput").ap()
    build(nc, *args, y)
    r = run(nc, [arrays], core_ids=[0])
    return r.results[0]["y"]
```

```python
from contextlib import ExitStack

import concourse.bass as bass
from concourse import mybir

F32, I32, U32, BF16 = mybir.dt.float32, mybir.dt.int32, mybir.dt.uint32, mybir.dt.bfloat16
ALU, ACT, AX = mybir.AluOpType, mybir.ActivationFunctionType, mybir.AxisListType

P = 128
N = 8192
F = 64
TILES = N // P
PAIRS = TILES // 2
ROW = F + 2
SCORE_COL, OWN_COL = F, F + 1
MEAN_ROW = N
SKIP = 1 << 20
SLOTS = 16
ALWAYS = 4
STEPS = (4, 5, 6, 7, 8, 10, 12, 16)
SEGS = (0, 512, 2048, 4608, 8192)
NSEG = len(SEGS) - 1
FOUND = 8 * NSEG
PARTS = 4
PART = N // PARTS
G4 = 4
GROUPS = TILES // G4
ALPHA, NEG, EPS = 0.2, -9000000000000000.0, 1e-5


def build(nc, x, adj, w0, a0, w1, a1, out):
    tabs = [nc.dram_tensor(f"table{l}", (N + 1, ROW), F32, kind="Internal").ap() for l in range(2)]
    scores_row = [nc.dram_tensor(f"scores{l}", (N,), F32, kind="Internal").ap() for l in range(2)]
    wh_cols = [nc.dram_tensor(f"wh_columns{l}", (F, N), F32, kind="Internal").ap() for l in range(2)]

    with ExitStack() as ctx:
        def sb(name, shape, dt=F32):
            return ctx.enter_context(nc.sbuf_tensor(name, shape, dt))

        def sem(name):
            return ctx.enter_context(nc.semaphore(name))

        ring = [sb(f"ring{b}", [P, N], I32) for b in range(2)]
        ringf = [r[:, :].bitcast(F32) for r in ring]
        both_signs = sb("both_signs", [P, 2 * (N + FOUND)], BF16)
        signs = [both_signs[:, b * (N + FOUND):(b + 1) * (N + FOUND)] for b in range(2)]
        feature = both_signs[:, 0:2 * N].bitcast(F32)
        xs = sb("xs", [P, TILES * F])
        acc = sb("acc", [P, TILES * F])
        wh = sb("wh", [P, TILES * ROW])
        both_G = sb("both_G", [P, 4 * SLOTS * ROW])
        G = [both_G[:, b * 2 * SLOTS * ROW:(b + 1) * 2 * SLOTS * ROW] for b in range(2)]
        scratch = both_G[:, 0:TILES * F]
        prod = sb("prod", [P, SLOTS * 2 * F])
        lists = sb("lists", [P, TILES * SLOTS], U32)
        slot_idx = [sb(f"slot_idx{b}", [P, 2 * SLOTS], U32) for b in range(2)]
        hst = [sb(f"hst{b}", [P, G4 * F]) for b in range(2)]
        hT = [sb(f"hT{b}", [F, G4 * P]) for b in range(2)]
        pT = [sb(f"pT{b}", [P, G4 * P]) for b in range(2)]
        ident = sb("ident", [P, P])
        ones8 = sb("ones8", [P, 8], BF16)
        over_n = sb("over_n", [P, 1])
        seg_base = sb("seg_base", [P, 2 * FOUND])
        seg_len = sb("seg_len", [P, 2 * FOUND])
        none_at = sb("none_at", [P, 2 * SLOTS])
        found = sb("found", [P, 2 * FOUND], U32)
        key0 = sb("key0", [P, 2 * FOUND])
        valid = sb("valid", [P, 2 * FOUND])
        key = sb("key", [P, 2 * FOUND])
        top = sb("top", [P, 2 * SLOTS])
        gap = sb("gap", [P, 2 * SLOTS])
        degree = [sb(f"degree{b}", [P, 2]) for b in range(2)]
        degree_max = sb("degree_max", [P, 2])
        last_key = sb("last_key", [P, 1])
        seg_over = sb("seg_over", [P, 1])
        over = sb("over", [P, 1])
        counts = sb("counts", [1, TILES], I32)
        flag = sb("flag", [1, 1], I32)
        z = sb("z", [P, 2 * SLOTS])
        e = [sb(f"e{b}", [P, 2 * SLOTS]) for b in range(2)]
        pen = sb("pen", [P, 2 * SLOTS])
        rowmax = sb("rowmax", [P, 2])
        pexp = [sb(f"pexp{b}", [P, 2 * SLOTS]) for b in range(2)]
        pw = sb("pw", [P, 2 * SLOTS])
        sums = sb("sums", [P, TILES])
        rsums = sb("rsums", [P, TILES])
        mean = sb("mean", [P, TILES])
        var = sb("var", [P, TILES])
        std = sb("std", [P, TILES])
        rstd = sb("rstd", [P, TILES])
        mean_wh = sb("mean_wh", [1, ROW])
        scores_t = sb("scores_t", [TILES, P])
        dense_max = sb("dense_max", [P, 1])
        dense_neg = sb("dense_neg", [P, 1])
        dense_sum = sb("dense_sum", [P, 1])
        dense_acc = sb("dense_acc", [P, F])
        w_in = [sb(f"w_in{l}", [F, F]) for l in range(2)]
        a_in = [sb(f"a_in{l}", [F, 2]) for l in range(2)]
        w_t = [sb(f"w_t{l}", [F, F]) for l in range(2)]
        wx = [sb(f"wx{l}", [F, ROW]) for l in range(2)]

        def ps(name):
            return ctx.enter_context(nc.psum_tensor(name, [P, 512], F32))

        psT = [ps(f"psT{b}") for b in range(2)]
        psW = [ps(f"psW{b}") for b in range(2)]
        psS = [ps(f"psS{b}") for b in range(2)]
        psD = [ps(f"psD{b}") for b in range(2)]

        x_landed = sem("x_landed")
        w_landed = sem("w_landed")
        consts = sem("consts")
        consts0 = sem("consts0")
        zeroed = sem("zeroed")
        sentinels_set = sem("sentinels_set")
        passed = [sem(f"passed_{name}") for name in ("pe", "pool", "dve")]
        w_turned = sem("w_turned")
        wt_copied = sem("wt_copied")
        a_through = sem("a_through")
        wx_ready = sem("wx_ready")
        var_ready = sem("var_ready")
        std_ready = sem("std_ready")
        h_ready = sem("h_ready")
        h_turned = sem("h_turned")
        hT_ready = sem("hT_ready")
        wh_done = sem("wh_done")
        wh_copied = sem("wh_copied")
        mean_summed = sem("mean_summed")
        mean_ready = sem("mean_ready")
        table_stored = sem("table_stored")
        dense_landed = sem("dense_landed")
        dense_added = sem("dense_added")
        dense_scored = sem("dense_scored")
        dense_exped = sem("dense_exped")
        p_turned = sem("p_turned")
        pT_ready = sem("pT_ready")
        dense_block = sem("dense_block")
        dense_copied = sem("dense_copied")
        adj_landed = [sem(f"adj_landed{b}") for b in range(2)]
        signed = [sem(f"signed{c}") for c in range(2)]
        searched = [sem(f"searched{c}") for c in range(2)]
        listed = sem("listed")
        degrees_turned = sem("degrees_turned")
        counted = sem("counted")
        idx_copied = sem("idx_copied")
        neighbours_in = sem("neighbours_in")
        gathered = [sem(f"gathered{b}") for b in range(2)]
        scored = sem("scored")
        exped = sem("exped")
        weighted = sem("weighted")
        summed = sem("summed")
        acc_copied = sem("acc_copied")
        over_ready = sem("over_ready")
        over_turned = sem("over_turned")
        flag_ready = sem("flag_ready")
        neg_ready = sem("neg_ready")
        elu_exped = sem("elu_exped")
        y_ready = sem("y_ready")
        out_stored = sem("out_stored")
        g_column = [sem(f"g_column{l}") for l in range(2)]
        g_landed = [sem(f"g_landed{l}") for l in range(2)]
        g_added = [sem(f"g_added{l}") for l in range(2)]
        g_scored = [sem(f"g_scored{l}") for l in range(2)]
        g_exped = [sem(f"g_exped{l}") for l in range(2)]
        g_feature = [sem(f"g_feature{l}") for l in range(2)]
        g_used = [sem(f"g_used{l}") for l in range(2)]

        def past(n, least):
            return not isinstance(n, int) or n >= least

        def stand_alone(eng, which):
            eng.sem_inc(passed[which], 1)

        def tile_rows(t):
            return bass.ds(t * P, P) if not isinstance(t, int) else slice(t * P, (t + 1) * P)

        def cols(t, w):
            return bass.ds(t * w, w) if not isinstance(t, int) else slice(t * w, (t + 1) * w)

        def pairs(eng, body, peel):
            for p in range(peel):
                body(p, p % 2)
            with eng.Fori(peel // 2, PAIRS // 2) as i:
                for b in range(2):
                    body(i * 2 + b, b)

        def tiles_of(p):
            return (1,) if isinstance(p, int) and p == 0 else (0, 1)

        def of_c(p, c):
            return p + c

        def groups(eng, body):
            for g in range(2):
                body(g, g)
            with eng.Fori(1, GROUPS // 2) as i:
                for b in range(2):
                    body(i * 2 + b, b)

        block = ctx.enter_context(nc.Block())

        @block.sync
        def _(sp):
            sp.dma_start(w_in[0][:, :], w0).then_inc(w_landed, 16)
            sp.dma_start(w_in[1][:, :], w1).then_inc(w_landed, 16)
            for l, a in enumerate((a0, a1)):
                sp.dma_start(a_in[l][:, 0:1], a[F:2 * F, :]).then_inc(w_landed, 16)
                sp.dma_start(a_in[l][:, 1:2], a[0:F, :]).then_inc(w_landed, 16)
            sp.dma_start(xs[:, :].rearrange("p (t f) -> p t f", f=F),
                         x.rearrange("(t p) f -> p t f", p=P)).then_inc(x_landed, 16)

            def store_table(l):
                sp.wait_ge(wh_copied, GROUPS * (l + 1))
                whv = wh[:, :].rearrange("p (t c) -> p t c", c=ROW)
                sp.dma_start(tabs[l][0:N, :].rearrange("(t p) c -> p t c", p=P), whv).then_inc(table_stored, 16)
                sp.wait_ge(mean_ready, l + 1)
                sp.dma_start(scores_row[l].rearrange("(t p) -> t p", p=P), scores_t[:, :]).then_inc(table_stored, 16)
                sp.dma_start(tabs[l][N:N + 1, :], mean_wh[:, :]).then_inc(table_stored, 16)

            def load_dense(l):
                if l == 0:
                    sp.wait_ge(signed[0], PAIRS - 1)
                sp.dma_start(ring[0][:, :], adj[0:P, :]).then_inc(dense_landed, 16)
                if l == 0:
                    sp.wait_ge(signed[1], PAIRS)
                else:
                    store_table(1)
                    sp.wait_ge(table_stored, 96)
                sp.dma_start(ringf[1], scores_row[l].rearrange("(a n) -> a n", a=1).broadcast_to([P, N]))\
                    .then_inc(dense_landed, 16)

            def load(p, b):
                for c in tiles_of(p):
                    if past(p, 2 - c):
                        sp.wait_ge(signed[c], of_c(p, c) - 1)
                    for part in range(PARTS):
                        sp.dma_start(ring[c][:, part * PART:(part + 1) * PART],
                                     adj[tile_rows(p * 2 + c), part * PART:(part + 1) * PART]).then_inc(adj_landed[c], 16)
                if isinstance(p, int) and p == 1:
                    store_table(0)
                    sp.wait_ge(table_stored, 48)

            pairs(sp, load, 4)
            load_dense(0)
            sp.wait_ge(y_ready, 1)
            load_dense(1)
            sp.wait_ge(y_ready, 2)
            sp.dma_start(out.rearrange("(t p) f -> p t f", p=P),
                         xs[:, :].rearrange("p (t f) -> p t f", f=F)).then_inc(out_stored, 16)
            sp.wait_ge(out_stored, 16)

        @block.gpsimd
        def _(pool):
            pool.memset(ident[:, :], 0.0).then_inc(consts0, 1)
            pool.wait_ge(consts0, 1)
            pool.affine_select(out=ident[:, :], in_=ident[:, :], compare_op=ALU.not_equal, fill=1.0,
                               base=0, pattern=[[-1, P]], channel_multiplier=1).then_inc(consts, 1)
            pool.wait_ge(var_ready, 1)
            pool.memset(both_G[:, :], 0.0).then_inc(zeroed, 1)
            pool.wait_ge(zeroed, 1)
            regs = [pool.alloc_register(f"most_edges{c}") for c in range(2)]
            landing = [pool.alloc_register(f"landing{b}") for b in range(2)]
            for b in range(2):
                pool.reg_mov(landing[b], 0)

            def all_in(b):
                pool.wait_ge(gathered[b], pool.snap(landing[b], min_val=0, max_val=1 << 15))
                pool.sem_inc(neighbours_in, 1)

            def gather(l, p, b):
                at = PAIRS * l + p
                if l == 0:
                    pool.wait_ge(counted, p + 1)
                if past(at, 2):
                    pool.wait_ge(weighted, at - 1)
                pool.tensor_copy(slot_idx[b][:, :], lists[:, cols(p, 2 * SLOTS)]).then_inc(idx_copied, 1)
                most = {}
                for c in tiles_of(p):
                    pool.reg_load(regs[c], counts[0:1, cols(p * 2 + c, 1)])
                    most[c] = pool.snap(regs[c], min_val=0, max_val=FOUND)
                pool.wait_ge(idx_copied, at + 1)
                stand_alone(pool, 1)

                def slots(c, first, last):
                    for k in range(c * SLOTS + first, c * SLOTS + last):
                        pool.indirect_dma_start(
                            out=G[b][:, k * ROW:(k + 1) * ROW], out_offset=None, in_=tabs[l],
                            in_offset=bass.IndirectOffsetOnAxis(ap=slot_idx[b][:, k:k + 1], axis=0),
                            bounds_check=MEAN_ROW, oob_is_err=False).then_inc(gathered[b], 16)

                for c in tiles_of(p):
                    slots(c, 0, ALWAYS)
                    pool.reg_add(landing[b], landing[b], 16 * ALWAYS)
                    if l == 1 and past(p, 1) and c == tiles_of(p)[0]:
                        all_in(1 - b)
                    for first, last in zip(STEPS, STEPS[1:]):
                        with pool.If(most[c] > first):
                            slots(c, first, last)
                            pool.reg_add(landing[b], landing[b], 16 * (last - first))
                        with pool.Else():
                            pool.nop()
                if l == 0:
                    all_in(b)

            for l in range(2):
                pool.wait_ge(table_stored, 48 * (l + 1))
                pairs(pool, lambda p, b: gather(l, p, b), 2)
            all_in(1)

        @block.scalar
        def _(act):
            act.wait_ge(w_turned, 2)
            for l in range(2):
                act.activation(w_t[l][:, :], psT[l][0:F, 0:F], ACT.Copy).then_inc(wt_copied, 1)
            act.wait_ge(a_through, 2)
            act.wait_ge(wt_copied, 2)
            act.activation(wx[0][:, 0:F], w_t[0][:, :], ACT.Copy).then_inc(wx_ready, 1)
            act.wait_ge(w_landed, 96)
            act.activation(wx[1][:, 0:F], w_in[1][:, :], ACT.Copy).then_inc(wx_ready, 1)
            for l in range(2):
                act.activation(wx[l][:, F:ROW], psW[l][0:F, 0:2], ACT.Copy).then_inc(wx_ready, 1)

            def features(l):
                act.wait_ge(var_ready, l + 1)
                act.activation(std[:, :], var[:, :], ACT.Sqrt).then_inc(std_ready, 1)

                def copy_rows(g, b):
                    act.wait_ge(wh_done, GROUPS * l + g + 1)
                    act.activation(wh[:, cols(g, G4 * ROW)], psW[b][:, 0:G4 * ROW], ACT.Copy).then_inc(wh_copied, 1)

                def group(g, b):
                    at = GROUPS * l + g
                    act.wait_ge(h_turned, at + 1)
                    if past(at, 2):
                        act.wait_ge(wh_done, at - 1)
                    act.activation(hT[b][:, :], psT[b][0:F, :], ACT.Copy).then_inc(hT_ready, 1)
                    if past(g, 1):
                        copy_rows(g - 1, 1 - b)

                groups(act, group)
                copy_rows(GROUPS - 1, 1)

            def dense_exp(l):
                act.wait_ge(dense_landed, 32 * (l + 1))
                act.activation(ringf[1], ringf[1], ACT.Identity, bias=wh[:, OWN_COL:ROW])\
                    .then_inc(dense_added, 1)
                act.wait_ge(dense_scored, l + 1)
                act.activation(ringf[1], ringf[1], ACT.Exp, bias=dense_neg[:, :],
                               accum_out=dense_sum[:, :]).then_inc(dense_exped, 1)

            def dense_turn(l):
                for q in range(GROUPS):
                    at = GROUPS * l + q
                    act.wait_ge(p_turned, at + 1)
                    if past(at, 2):
                        act.wait_ge(dense_block, at - 1)
                    act.activation(pT[q % 2][:, :], psT[q % 2][:, :], ACT.Copy).then_inc(pT_ready, 1)
                act.wait_ge(dense_block, GROUPS * (l + 1))
                act.activation(dense_acc[:, :], psW[0][:, 0:F], ACT.Copy).then_inc(dense_copied, 1)

            def exp(l, p, b):
                act.wait_ge(scored, PAIRS * l + p + 1)
                act.activation(pexp[b][:, :], e[b][:, :], ACT.Exp).then_inc(exped, 1)

            def copy_sum(l, p, b):
                act.wait_ge(summed, PAIRS * l + p + 1)
                act.activation(acc[:, cols(p, 2 * F)], psS[b][:, 0:2 * F], ACT.Copy).then_inc(acc_copied, 1)

            def sign(p, b):
                for c in tiles_of(p):
                    act.wait_ge(adj_landed[c], of_c(p, c) * (16 * PARTS))
                    if past(p, 2 - c):
                        act.wait_ge(searched[c], of_c(p, c) - 1)
                    for s in range(NSEG):
                        lo, hi = SEGS[s], SEGS[s + 1]
                        done = act.activation(signs[c][:, lo + 8 * s:hi + 8 * s], ring[c][:, lo:hi], ACT.Sign)
                        if s == 2 and c == 0 and past(p, 3):
                            exp(0, p - 3, 1 - b)
                    done.then_inc(signed[c], 1)
                if past(p, 4):
                    copy_sum(0, p - 4, b)

            def general(l):
                reg = act.alloc_register(f"act_flag{l}")
                act.wait_ge(flag_ready, 1)
                act.wait_ge(g_used[l], 1)
                act.reg_load(reg, flag[0:1, 0:1])
                some = act.snap(reg, min_val=0, max_val=N)
                with act.If(some > 0):
                    with act.Fori(0, F) as f:
                        act.dma_start(wh_cols[l][bass.ds(f, 1), :],
                                      tabs[l][0:N, bass.ds(f, 1)].rearrange("n a -> a n"),
                                      allow_slow_non_contiguous=True).then_inc(g_column[l], 16)
                        act.wait_ge(g_column[l], f * 16 + 16)
                    with act.Fori(0, TILES) as t:
                        act.wait_ge(g_used[l], t * (F + 1) + 1)
                        act.dma_start(ring[0][:, :], adj[bass.ds(t * P, P), :]).then_inc(g_landed[l], 16)
                        act.dma_start(ringf[1], scores_row[l].rearrange("(a n) -> a n", a=1).broadcast_to([P, N]))\
                            .then_inc(g_landed[l], 16)
                        act.wait_ge(g_landed[l], t * 32 + 32)
                        act.activation(ringf[1], ringf[1], ACT.Identity,
                                       bias=wh[:, bass.ds(t * ROW + OWN_COL, 1)]).then_inc(g_added[l], 1)
                        act.wait_ge(g_scored[l], t + 1)
                        act.activation(ringf[1], ringf[1], ACT.Exp, bias=dense_neg[:, :],
                                       accum_out=dense_sum[:, :]).then_inc(g_exped[l], 1)
                        with act.Fori(0, F) as f:
                            act.wait_ge(g_used[l], t * (F + 1) + f + 1)
                            act.dma_start(feature[:, :], wh_cols[l][bass.ds(f, 1), :].broadcast_to([P, N]))\
                                .then_inc(g_feature[l], 16)
                with act.Else():
                    act.nop()

            def elu(l):
                act.wait_ge(neg_ready, l + 1)
                act.activation(scratch, scratch, ACT.Exp).then_inc(elu_exped, 1)

            act.wait_ge(sentinels_set, 1)
            sign(0, 0)
            features(0)
            for p in range(1, 4):
                sign(p, p % 2)
            with act.Fori(2, PAIRS // 2) as i:
                for b in range(2):
                    sign(i * 2 + b, b)
            exp(0, PAIRS - 3, 1)
            copy_sum(0, PAIRS - 4, 0)
            exp(0, PAIRS - 2, 0)
            copy_sum(0, PAIRS - 3, 1)
            dense_exp(0)
            exp(0, PAIRS - 1, 1)
            copy_sum(0, PAIRS - 2, 0)
            dense_turn(0)
            copy_sum(0, PAIRS - 1, 1)
            general(0)
            elu(0)
            features(1)
            dense_exp(1)
            dense_turn(1)

            def second(p, b):
                exp(1, p, b)
                if past(p, 1):
                    copy_sum(1, p - 1, 1 - b)

            pairs(act, second, 2)
            copy_sum(1, PAIRS - 1, 1)
            general(1)
            elu(1)

        @block.tensor
        def _(pe):
            pe.wait_ge(consts, 1)
            pe.wait_ge(sentinels_set, 1)
            pe.wait_ge(w_landed, 96)
            for l in range(2):
                pe.transpose(psT[l][0:F, 0:F], w_in[l][:, :], ident[0:F, 0:F]).then_inc(w_turned, 1)
            pe.matmul(psW[0][0:F, 0:2], w_in[0][:, :], a_in[0][:, :], start=True, stop=True).then_inc(a_through, 1)
            pe.wait_ge(wt_copied, 2)
            pe.matmul(psW[1][0:F, 0:2], w_t[1][:, :], a_in[1][:, :], start=True, stop=True).then_inc(a_through, 1)
            pe.wait_ge(wx_ready, 4)

            def features(l):
                def multiply(g, b):
                    at = GROUPS * l + g
                    pe.wait_ge(hT_ready, at + 1)
                    if past(at, 2):
                        pe.wait_ge(wh_copied, at - 1)
                    for k in range(G4):
                        done = pe.matmul(psW[b][:, k * ROW:(k + 1) * ROW], hT[b][:, k * P:(k + 1) * P],
                                         wx[l][:, :], start=True, stop=True)
                    done.then_inc(wh_done, 1)

                def group(g, b):
                    at = GROUPS * l + g
                    pe.wait_ge(h_ready, at + 1)
                    if past(at, 2):
                        pe.wait_ge(hT_ready, at - 1)
                        stand_alone(pe, 0)
                    for k in range(G4):
                        done = pe.transpose(psT[b][0:F, k * P:(k + 1) * P], hst[b][:, k * F:(k + 1) * F], ident[:, :])
                    done.then_inc(h_turned, 1)
                    if past(g, 1):
                        multiply(g - 1, 1 - b)

                groups(pe, group)
                multiply(GROUPS - 1, 1)
                pe.wait_ge(wh_copied, GROUPS * (l + 1))
                for q in range(GROUPS):
                    done = pe.matmul(psD[1][0:1, 0:G4 * ROW], over_n[:, :], wh[:, q * G4 * ROW:(q + 1) * G4 * ROW],
                                     start=(q == 0), stop=(q == GROUPS - 1))
                if l:
                    pe.wait_ge(flag_ready, l)
                scores = wh[:, :].rearrange("p (t c) -> p t c", c=ROW)[:, :, SCORE_COL]
                done = pe.matmul(psD[0][0:TILES, 0:P], scores, ident[:, :], start=True, stop=True)
                done.then_inc(mean_summed, 1)

            def dense(l):
                pe.wait_ge(dense_exped, l + 1)
                pe.wait_ge(wh_copied, GROUPS * (l + 1))
                for q in range(GROUPS + 1):
                    if q < GROUPS:
                        if past(GROUPS * l + q, 2):
                            pe.wait_ge(pT_ready, GROUPS * l + q - 1)
                        for k in range(G4):
                            j = q * G4 + k
                            done = pe.transpose(psT[q % 2][:, k * P:(k + 1) * P], ringf[1][:, j * P:(j + 1) * P], ident[:, :])
                        done.then_inc(p_turned, 1)
                    if q > 0:
                        pe.wait_ge(pT_ready, GROUPS * l + q)
                        for k in range(G4):
                            j = (q - 1) * G4 + k
                            done = pe.matmul(psW[0][:, 0:F], pT[(q - 1) % 2][:, k * P:(k + 1) * P],
                                             wh[:, j * ROW:j * ROW + F], start=(j == 0), stop=(j == TILES - 1))
                        done.then_inc(dense_block, 1)

            def turn_degrees(p, b):
                pe.wait_ge(listed, p + 1)
                if past(p, 2):
                    pe.wait_ge(counted, p - 1)
                for c in range(2):
                    done = pe.matmul(psD[b][0:1, c * P:(c + 1) * P], degree[b][:, c:c + 1], ident[:, :],
                                     start=True, stop=True)
                done.then_inc(degrees_turned, 1)

            def sum_slots(l, p, b):
                pe.wait_ge(weighted, PAIRS * l + p + 1)
                if past(PAIRS * l + p, 2):
                    pe.wait_ge(acc_copied, PAIRS * l + p - 1)
                for k in range(SLOTS):
                    done = pe.matmul(psS[b][:, 0:2 * F], ident[:, :], prod[:, k * 2 * F:(k + 1) * 2 * F],
                                     start=(k == 0), stop=(k == SLOTS - 1))
                done.then_inc(summed, 1)

            def first(p, b):
                turn_degrees(p, b)
                if past(p, 2):
                    sum_slots(0, p - 2, b)

            features(0)
            pe.wait_ge(mean_ready, 1)
            pairs(pe, first, 4)
            sum_slots(0, PAIRS - 2, 0)
            dense(0)
            sum_slots(0, PAIRS - 1, 1)
            pe.wait_ge(over_ready, 1)
            pe.matmul(psD[0][0:1, 0:P], over[:, :], ident[:, :], start=True, stop=True).then_inc(over_turned, 1)
            features(1)
            dense(1)
            pairs(pe, lambda p, b: sum_slots(1, p, b), 2)

        @block.vector
        def _(dve):
            dve.memset(ones8[:, :], 1.0)
            dve.memset(over_n[:, :], 1.0 / N)
            for c in range(2):
                for s in range(NSEG):
                    at = c * FOUND + 8 * s
                    dve.memset(seg_base[:, at:at + 8], float(SEGS[s] + 1))
                    dve.memset(seg_len[:, at:at + 8], float(SEGS[s + 1] - SEGS[s]))
                    end = SEGS[s + 1] + 8 * s
                    dve.memset(signs[c][:, end:end + 8], 1.0)
                dve.memset(none_at[:, c * SLOTS:c * SLOTS + 1], float(MEAN_ROW + 1))
                dve.memset(none_at[:, c * SLOTS + 1:(c + 1) * SLOTS], float(SKIP))
            dve.memset(found[:, :], N)
            dve.memset(degree_max[:, :], 0.0)
            dve.memset(seg_over[:, :], 0.0)
            dve.drain()
            dve.memset(pw[:, :], 0.0).then_inc(sentinels_set, 1)

            xv = xs[:, :].rearrange("p (t f) -> p t f", f=F)
            av = acc[:, :].rearrange("p (t f) -> p t f", f=F)
            whv = wh[:, :].rearrange("p (t c) -> p t c", c=ROW)
            sq = scratch
            sqv = sq.rearrange("p (t f) -> p t f", f=F)

            def over_features(v):
                return v[:, :].rearrange("p (t a) -> p t a", a=1).broadcast_to([P, TILES, F])

            def features(l):
                if l == 0:
                    dve.wait_ge(x_landed, 16)
                dve.tensor_reduce(mean[:, :], xv, AX.X, ALU.add)
                dve.drain()
                dve.tensor_scalar(mean[:, :], mean[:, :], 1.0 / F, None, ALU.mult)
                dve.drain()
                dve.tensor_tensor(av, xv, over_features(mean), ALU.subtract)
                dve.drain()
                dve.tensor_tensor(sq, acc[:, :], acc[:, :], ALU.mult)
                dve.drain()
                dve.tensor_reduce(var[:, :], sqv, AX.X, ALU.add)
                dve.drain()
                dve.tensor_scalar(var[:, :], var[:, :], 1.0 / F, EPS, ALU.mult, ALU.add).then_inc(var_ready, 1)
                dve.wait_ge(std_ready, l + 1)
                dve.reciprocal(rstd[:, :], std[:, :])
                dve.drain()

                def group(g, b):
                    if past(GROUPS * l + g, 2):
                        dve.wait_ge(h_turned, GROUPS * l + g - 1)
                    r = rstd[:, cols(g, G4)].rearrange("p (t a) -> p t a", a=1).broadcast_to([P, G4, F])
                    dve.scalar_tensor_tensor(hst[b][:, :].rearrange("p (t f) -> p t f", f=F),
                                             acc[:, cols(g, G4 * F)].rearrange("p (t f) -> p t f", f=F),
                                             0.0, r, ALU.max, ALU.mult).then_inc(h_ready, 1)

                groups(dve, group)

            def finish_table(l):
                dve.wait_ge(mean_summed, l + 1)
                dve.tensor_copy(scores_t[:, :], psD[0][0:TILES, 0:P])
                dve.drain()
                dve.tensor_reduce(mean_wh[:, :], psD[1][0:1, 0:G4 * ROW].rearrange("p (k c) -> p c k", c=ROW),
                                  AX.X, ALU.add).then_inc(mean_ready, 1)

            def dense_scores(added, count):
                dve.tensor_scalar(ringf[0], ring[0][:, :], 0, NEG, ALU.is_le, ALU.mult)
                dve.drain()
                dve.wait_ge(added, count)
                dve.scalar_tensor_tensor(ringf[1], ringf[1], ALPHA, ringf[1], ALU.mult, ALU.max)
                dve.drain()
                dve.tensor_tensor_reduce(ringf[1], ringf[1], ringf[0], 1.0, NEG, ALU.add, ALU.max, dense_max[:, :])
                dve.drain()
                return dve.tensor_scalar(dense_neg[:, :], dense_max[:, :], -1.0, None, ALU.mult)

            def dense(l):
                dve.wait_ge(dense_landed, 32 * (l + 1))
                dense_scores(dense_added, l + 1).then_inc(dense_scored, 1)

            def search(c):
                for s in range(NSEG):
                    at = c * FOUND + 8 * s
                    done = dve.max_index(found[:, at:at + 8], ones8[:, :],
                                         signs[c][:, SEGS[s] + 8 * s:SEGS[s + 1] + 8 * s + 8])
                done.then_inc(searched[c], 1)

            def by_tile(v):
                return v[:, :].rearrange("p (c k) -> p c k", c=2)

            def make_lists(p, b):
                dve.drain()
                dve.tensor_tensor(key0[:, :], found[:, :], seg_base[:, :], ALU.add)
                dve.tensor_tensor(valid[:, :], found[:, :], seg_len[:, :], ALU.is_lt)
                dve.drain()
                dve.tensor_tensor(key[:, :], key0[:, :], valid[:, :], ALU.mult)
                dve.tensor_reduce(degree[b][:, :], by_tile(valid), AX.X, ALU.add)
                dve.drain()
                for c in range(2):
                    dve.max(top[:, c * SLOTS:c * SLOTS + 8], key[:, c * FOUND:(c + 1) * FOUND])
                dve.tensor_reduce(last_key[:, :], valid[:, 7:2 * FOUND:8], AX.X, ALU.max)
                dve.drain()
                for c in range(2):
                    dve.match_replace(key0[:, c * FOUND:(c + 1) * FOUND], top[:, c * SLOTS:c * SLOTS + 8],
                                      key[:, c * FOUND:(c + 1) * FOUND], 0.0)
                dve.tensor_tensor(seg_over[:, :], seg_over[:, :], last_key[:, :], ALU.max)
                dve.tensor_tensor(degree_max[:, :], degree_max[:, :], degree[b][:, :], ALU.max)
                dve.drain()
                for c in range(2):
                    dve.max(top[:, c * SLOTS + 8:(c + 1) * SLOTS], key0[:, c * FOUND:(c + 1) * FOUND])
                dve.drain()
                dve.scalar_tensor_tensor(gap[:, :], top[:, :], 0.0, none_at[:, :], ALU.is_equal, ALU.mult)
                dve.drain()
                dve.scalar_tensor_tensor(lists[:, cols(p, 2 * SLOTS)], top[:, :], -1.0, gap[:, :], ALU.add, ALU.add)\
                    .then_inc(listed, 1)

            def count(p, b):
                dve.wait_ge(degrees_turned, p + 1)
                dve.tensor_reduce(counts[0:1, cols(p, 2)], psD[b][0:1, 0:2 * P].rearrange("p (c r) -> p c r", c=2),
                                  AX.X, ALU.max).then_inc(counted, 1)

            def score(l, p, b):
                dve.wait_ge(neighbours_in, PAIRS * l + p + 1)
                gathered_rows = G[b].rearrange("p (c k r) -> p c k r", c=2, r=ROW)
                own = wh[:, cols(p, 2 * ROW)].rearrange("p (c r) -> p c r", c=2)[:, :, OWN_COL:ROW]
                dve.tensor_tensor(by_tile(z), gathered_rows[:, :, :, SCORE_COL], own.broadcast_to([P, 2, SLOTS]), ALU.add)
                dve.tensor_scalar(pen[:, :], slot_idx[b][:, :], float(MEAN_ROW), NEG, ALU.is_gt, ALU.mult)
                dve.drain()
                dve.scalar_tensor_tensor(z[:, :], z[:, :], ALPHA, z[:, :], ALU.mult, ALU.max)
                dve.drain()
                dve.tensor_tensor(z[:, :], z[:, :], pen[:, :], ALU.add)
                dve.drain()
                dve.tensor_reduce(rowmax[:, :], by_tile(z), AX.X, ALU.max)
                dve.drain()
                dve.tensor_tensor(by_tile(e[b]), by_tile(z),
                                  rowmax[:, :].rearrange("p (c a) -> p c a", a=1).broadcast_to([P, 2, SLOTS]),
                                  ALU.subtract).then_inc(scored, 1)

            def weigh(l, p, b):
                dve.wait_ge(exped, PAIRS * l + p + 1)
                dve.scalar_tensor_tensor(pw[:, :], slot_idx[b][:, :], float(MEAN_ROW), pexp[b][:, :],
                                         ALU.is_le, ALU.mult)
                dve.drain()
                if past(PAIRS * l + p, 1):
                    dve.wait_ge(summed, PAIRS * l + p)
                for c in range(2):
                    rows = G[b].rearrange("p (c k r) -> p c k r", c=2, r=ROW)
                    w = pw[:, c * SLOTS:(c + 1) * SLOTS].rearrange("p (k a) -> p k a", a=1)
                    done = dve.tensor_tensor(prod[:, :].rearrange("p (k c f) -> p c k f", c=2, f=F)[:, c],
                                             rows[:, c, :, 0:F], w.broadcast_to([P, SLOTS, F]), ALU.mult)
                done.then_inc(weighted, 1)
                dve.tensor_reduce(sums[:, cols(p, 2)], by_tile(pw), AX.X, ALU.add)

            def stream(p, b):
                for c in tiles_of(p):
                    dve.wait_ge(signed[c], of_c(p, c))
                    stand_alone(dve, 2)
                    search(c)
                    if c == 0 and past(p, 2):
                        score(0, p - 2, b)
                if isinstance(p, int) and p == 0:
                    finish_table(0)
                make_lists(p, b)
                if past(p, 2):
                    weigh(0, p - 2, b)
                count(p, b)

            def general(l):
                reg = dve.alloc_register(f"dve_flag{l}")
                dve.wait_ge(flag_ready, 1)
                dve.drain()
                dve.reg_load(reg, flag[0:1, 0:1])
                some = dve.snap(reg, min_val=0, max_val=N)
                dve.drain().then_inc(g_used[l], 1)
                with dve.If(some > 0):
                    with dve.Fori(0, TILES) as t:
                        dve.wait_ge(g_landed[l], t * 32 + 32)
                        dense_scores(g_added[l], t + 1).then_inc(g_scored[l], 1)
                        dve.wait_ge(g_exped[l], t + 1)
                        dve.tensor_copy(sums[:, bass.ds(t, 1)], dense_sum[:, :])
                        with dve.Fori(0, F) as f:
                            dve.wait_ge(g_feature[l], (t * F + f) * 16 + 16)
                            dve.scalar_tensor_tensor(ringf[0], ringf[1], 1.0, feature[:, :], ALU.mult, ALU.mult,
                                                     accum_out=acc[:, bass.ds(t * F + f, 1)]).then_inc(g_used[l], 1)
                            dve.drain()
                        dve.drain().then_inc(g_used[l], 1)
                with dve.Else():
                    dve.nop()
                dve.drain()

            def residual(l):
                dve.reciprocal(rsums[:, :], sums[:, :])
                dve.drain()
                dve.tensor_tensor(av, av, over_features(rsums), ALU.mult)
                dve.drain()
                dve.tensor_scalar(scratch, acc[:, :], 0.0, None, ALU.min).then_inc(neg_ready, 1)
                dve.tensor_scalar(acc[:, :], acc[:, :], 0.0, None, ALU.max)
                dve.wait_ge(elu_exped, l + 1)
                dve.drain()
                dve.scalar_tensor_tensor(acc[:, :], scratch, -1.0, acc[:, :], ALU.add, ALU.add)
                dve.drain()
                dve.tensor_tensor(xs[:, :], xs[:, :], acc[:, :], ALU.add).then_inc(y_ready, 1)
                dve.drain()

            features(0)
            pairs(dve, stream, 4)
            score(0, PAIRS - 2, 0)
            weigh(0, PAIRS - 2, 0)
            dense(0)
            score(0, PAIRS - 1, 1)
            weigh(0, PAIRS - 1, 1)
            dve.tensor_reduce(over[:, :], degree_max[:, :], AX.X, ALU.max)
            dve.drain()
            dve.scalar_tensor_tensor(over[:, :], over[:, :], float(-SLOTS), seg_over[:, :], ALU.add, ALU.max)\
                .then_inc(over_ready, 1)
            dve.wait_ge(over_turned, 1)
            dve.tensor_reduce(flag[:, :], psD[0][0:1, 0:P], AX.X, ALU.max).then_inc(flag_ready, 1)

            def tile_0(l):
                dve.wait_ge(acc_copied, PAIRS * (l + 1))
                dve.wait_ge(dense_copied, l + 1)
                dve.tensor_copy(acc[:, 0:F], dense_acc[:, :])
                dve.tensor_copy(sums[:, 0:1], dense_sum[:, :])
                dve.drain()

            tile_0(0)
            general(0)
            residual(0)
            features(1)
            finish_table(1)
            dense(1)

            def second(p, b):
                score(1, p, b)
                weigh(1, p, b)

            pairs(dve, second, 2)
            tile_0(1)
            general(1)
            residual(1)


def kernel(**inputs):
    import numpy as np
    import concourse.bacc as bacc
    from concourse.bass_utils import run_bass_kernel_spmd as run

    names = ("x", "adj", "L0_gnn_W", "L0_gnn_a", "L1_gnn_W", "L1_gnn_a")
    nc = bacc.Bacc("TRN2", target_bir_lowering=False, num_devices=1)
    arrays, args = {}, []
    for name in names:
        a = np.ascontiguousarray(inputs[name])
        if name.endswith("_a"):
            a = a.reshape(2 * F, 1)
        arrays[f"in_{name}"] = a
        args.append(nc.dram_tensor(f"in_{name}", a.shape, mybir.dt.from_np(a.dtype), kind="ExternalInput").ap())
    y = nc.dram_tensor("y", (N, F), F32, kind="ExternalOutput").ap()
    build(nc, *args, y)
    r = run(nc, [arrays], core_ids=[0])
    return r.results[0]["y"]
```

```python
from contextlib import ExitStack

import concourse.bass as bass
from concourse import mybir

F32, I32, U32, BF16 = mybir.dt.float32, mybir.dt.int32, mybir.dt.uint32, mybir.dt.bfloat16
ALU, ACT, AX = mybir.AluOpType, mybir.ActivationFunctionType, mybir.AxisListType

P = 128
N = 8192
F = 64
TILES = N // P
PAIRS = TILES // 2
ROW = F + 2
SCORE_COL, OWN_COL = F, F + 1
MEAN_ROW = N
SKIP = 1 << 20
SLOTS = 24
RANGES = ((0, 4, 24), (4, 16, 16), (16, PAIRS, 12))
ALWAYS = 6
STEPS = (6, 7, 8, 9, 10, 11, 12, 13, 14, 16, 18, 19, 20, 22, 24)
QUADS = (2, 15)
EARLY, LATE = 2 * QUADS[0], 2 * QUADS[1]
LATER_SLOTS = 20
QUAD_FIRST = 3
QUAD_ALWAYS = 8
QUAD_STEPS = (8, 10, 11, 12, 13, 14, 15, 16, 17, 18, 19, 20, 21, 22, 24)
TURNED = QUADS[0] + 4
APART = 8
ELU_AT = {TURNED - 1: 0, TURNED: 1, QUADS[1] - 3: 2, QUADS[1] - 2: 3}
JOBS = (PAIRS, PAIRS + EARLY + QUADS[1] - QUADS[0] + PAIRS - LATE)
KEYS = N + 1
SEGS = (0, 512, 2048, 4608, 8192)
NSEG = len(SEGS) - 1
FOUND = 8 * NSEG
SEARCH = 2 * FOUND
WARMING = 28
PARTS = 4
PART = N // PARTS
G4 = 4
GROUPS = TILES // G4
CHUNKS = 4
CHUNK = TILES // CHUNKS
EQUAL = [(k * CHUNK, (k + 1) * CHUNK) for k in range(CHUNKS)]
STORES = 16 * (CHUNKS + 2)
TILE_0_LAST = [(1, CHUNK)] + EQUAL[1:] + [(0, 1)]
PIECES_1 = [(1, 16, PAIRS + EARLY + 1), (0, 1, None), (16, 32, PAIRS + EARLY + 5), (32, 48, PAIRS + EARLY + 9),
            (48, 60, PAIRS + EARLY + 12), (60, 64, JOBS[1] - 1)]
G_PIECE = len(TILE_0_LAST) + len(PIECES_1) + 1
ALPHA, NEG, EPS = 0.2, -9000000000000000.0, 1e-5


def build(nc, x, adj, w0, a0, w1, a1, out):
    tabs = [nc.dram_tensor(f"table{l}", (N + 1, ROW), F32, kind="Internal").ap() for l in range(2)]
    scores_row = [nc.dram_tensor(f"scores{l}", (N,), F32, kind="Internal").ap() for l in range(2)]
    wh_cols = [nc.dram_tensor(f"wh_columns{l}", (F, N), F32, kind="Internal").ap() for l in range(2)]

    with ExitStack() as ctx:
        def sb(name, shape, dt=F32):
            return ctx.enter_context(nc.sbuf_tensor(name, shape, dt))

        def sem(name):
            return ctx.enter_context(nc.semaphore(name))

        ring = [sb(f"ring{b}", [P, N], I32) for b in range(2)]
        ringf = [r[:, :].bitcast(F32) for r in ring]
        both_signs = sb("both_signs", [P, 2 * (N + FOUND)], BF16)
        signs = [both_signs[:, b * (N + FOUND):(b + 1) * (N + FOUND)] for b in range(2)]
        feature = both_signs[:, 0:2 * N].bitcast(F32)
        xs = sb("xs", [P, TILES * F])
        acc = sb("acc", [P, TILES * F])
        wh = sb("wh", [P, TILES * ROW])
        both_G = sb("both_G", [P, TILES * F])
        G = [both_G[:, b * SLOTS * ROW:(b + 1) * SLOTS * ROW] for b in range(2)]
        scratch = both_G[:, 0:TILES * F]
        scratch_1 = [ringf[0][:, (SLOTS * 4 + b * CHUNK) * F:(SLOTS * 4 + (b + 1) * CHUNK) * F] for b in range(2)]
        scratch_g = ringf[1][:, 0:TILES * F]
        quad_idx = [sb(f"quad_idx{b}", [P, SLOTS], U32) for b in range(2)]
        quad_pens = [sb(f"quad_pens{b}", [P, 4 * SLOTS]) for b in range(2)]
        quad_key = [sb(f"quad_key{i}", [P, 2 * SLOTS]) for i in range(2)]
        second_rows = sb("second_rows", [P, 2 * SLOTS])
        quad_top = sb("quad_top", [P, SLOTS])
        beyond = sb("beyond", [P, 5 * SLOTS])
        limits = sb("limits", [P, 5 * SLOTS])
        quad_counts = sb("quad_counts", [1, PAIRS // 2], I32)
        prod = sb("prod", [P, SLOTS * 2 * F])
        lists = sb("lists", [P, PAIRS * SLOTS], U32)
        pens = sb("pens", [P, PAIRS * 2 * SLOTS])
        slot_idx = [sb(f"slot_idx{b}", [P, SLOTS], U32) for b in range(2)]
        hst = [sb(f"hst{b}", [P, G4 * F]) for b in range(2)]
        hT = [sb(f"hT{b}", [P, G4 // 2 * P]) for b in range(2)]
        pT = [sb(f"pT{b}", [P, G4 * P]) for b in range(2)]
        quad_prod = [both_signs[:, 0:SLOTS * 8 * F].bitcast(F32), ringf[0][:, 0:SLOTS * 4 * F]]
        ident = sb("ident", [P, P])
        ones8 = sb("ones8", [P, 8], BF16)
        over_n = sb("over_n", [P, 1])
        seg_base = sb("seg_base", [P, SEARCH])
        seg_len = sb("seg_len", [P, SEARCH])
        mean_key = sb("mean_key", [P, 2])
        found = sb("found", [P, SEARCH], U32)
        place = sb("place", [P, SEARCH])
        valid = sb("valid", [P, SEARCH])
        key = [sb(f"key{i}", [P, SEARCH + 2]) for i in range(2)]
        top = sb("top", [P, SLOTS])
        gap = sb("gap", [P, SLOTS])
        of_second = sb("of_second", [P, SLOTS])
        shift = sb("shift", [P, SLOTS])
        degree = sb("degree", [P, 2])
        entries = sb("entries", [P, 2])
        length = [sb(f"length{b}", [P, 1]) for b in range(2)]
        last_key = sb("last_key", [P, 1])
        over = sb("over", [P, 1])
        counts = sb("counts", [1, PAIRS], I32)
        flag = sb("flag", [1, 1], I32)
        z = sb("z", [P, 4 * SLOTS])
        e = [sb(f"e{b}", [P, 4 * SLOTS]) for b in range(2)]
        rowmax = sb("rowmax", [P, 4])
        pexp = [sb(f"pexp{b}", [P, 4 * SLOTS]) for b in range(2)]
        sums = sb("sums", [P, TILES])
        rsums = sb("rsums", [P, TILES])
        row_sum = sb("row_sum", [P, TILES])
        var = sb("var", [P, TILES])
        std = sb("std", [P, TILES])
        rstd = sb("rstd", [P, TILES])
        tile_sum = sb("tile_sum", [P, G4 * ROW])
        mean_wh = sb("mean_wh", [1, ROW])
        scores_t = sb("scores_t", [TILES, P])
        dense_max = sb("dense_max", [P, 1])
        dense_neg = sb("dense_neg", [P, 1])
        dense_sums = sb("dense_sums", [P, PARTS])
        dense_sum = sb("dense_sum", [P, 1])
        dense_acc = sb("dense_acc", [P, F])
        w_in = [sb("w_in0", [F, 2 * F]), sb("w_in1", [2 * F, F])]
        w_t = [sb("w_t0", [2 * F, F]), sb("w_t1", [F, 2 * F])]
        a_in = [sb(f"a_in{l}", [F, 2]) for l in range(2)]
        wx = [sb(f"wx{l}", [2 * F, 2 * ROW]) for l in range(2)]

        def ps(name):
            return ctx.enter_context(nc.psum_tensor(name, [P, 512], F32))

        psT = [ps(f"psT{b}") for b in range(2)]
        psW = [ps(f"psW{b}") for b in range(2)]
        psS = [ps(f"psS{b}") for b in range(2)]
        psD = [ps(f"psD{b}") for b in range(2)]

        x_landed = [sem(f"x_landed{k}") for k in range(CHUNKS)]
        w_landed = sem("w_landed")
        consts = sem("consts")
        consts0 = sem("consts0")
        zeroed = sem("zeroed")
        sentinels_set = sem("sentinels_set")
        passed = [sem(f"passed_{name}") for name in ("pe", "pool", "dve")]
        w_turned = sem("w_turned")
        wt_copied = sem("wt_copied")
        a_through = sem("a_through")
        wx_ready = sem("wx_ready")
        wx_zeroed = sem("wx_zeroed")
        centred = sem("centred")
        squared = sem("squared")
        var_ready = sem("var_ready")
        std_ready = sem("std_ready")
        h_ready = sem("h_ready")
        h_turned = sem("h_turned")
        hT_ready = sem("hT_ready")
        wh_done = sem("wh_done")
        wh_copied = sem("wh_copied")
        tiles_added = sem("tiles_added")
        mean_summed = sem("mean_summed")
        mean_ready = sem("mean_ready")
        table_stored = sem("table_stored")
        dense_landed = sem("dense_landed")
        scores_landed = [sem(f"scores_landed{k}") for k in range(PARTS)]
        dense_added = sem("dense_added")
        dense_scored = sem("dense_scored")
        dense_exped = sem("dense_exped")
        p_turned = sem("p_turned")
        pT_ready = sem("pT_ready")
        dense_block = sem("dense_block")
        dense_copied = sem("dense_copied")
        adj_landed = [sem(f"adj_landed{b}") for b in range(2)]
        signed = [sem(f"signed{c}") for c in range(2)]
        searched = [sem(f"searched{c}") for c in range(2)]
        listed = sem("listed")
        lengths_turned = sem("lengths_turned")
        counted = sem("counted")
        quad_listed = sem("quad_listed")
        quad_lengths_turned = sem("quad_lengths_turned")
        quad_counted = sem("quad_counted")
        idx_copied = sem("idx_copied")
        neighbours_in = sem("neighbours_in")
        gathered = [sem(f"gathered{b}") for b in range(2)]
        scored = sem("scored")
        exped = sem("exped")
        weighted = sem("weighted")
        summed = sem("summed")
        acc_copied = sem("acc_copied")
        over_ready = sem("over_ready")
        over_turned = sem("over_turned")
        flag_ready = sem("flag_ready")
        scaled = sem("scaled")
        neg_ready = sem("neg_ready")
        elu_exped = sem("elu_exped")
        y_ready = sem("y_ready")
        out_stored = sem("out_stored")
        g_column = [sem(f"g_column{l}") for l in range(2)]
        g_landed = [sem(f"g_landed{l}") for l in range(2)]
        g_added = [sem(f"g_added{l}") for l in range(2)]
        g_scored = [sem(f"g_scored{l}") for l in range(2)]
        g_exped = [sem(f"g_exped{l}") for l in range(2)]
        g_feature = [sem(f"g_feature{l}") for l in range(2)]
        g_used = [sem(f"g_used{l}") for l in range(2)]

        def past(n, least):
            return not isinstance(n, int) or n >= least

        def stand_alone(eng, which):
            eng.sem_inc(passed[which], 1)

        def tile_rows(t):
            return bass.ds(t * P, P) if not isinstance(t, int) else slice(t * P, (t + 1) * P)

        def cols(t, w):
            return bass.ds(t * w, w) if not isinstance(t, int) else slice(t * w, (t + 1) * w)

        def pairs(eng, body, peel=RANGES[0][1], lag=0):
            before = RANGES[0][2]
            for first, last, slots in RANGES:
                apart = min(last, max(first + lag, peel))
                for p in range(first, apart):
                    body(p, p % 2, slots, before if p < first + lag else slots)
                if apart < last:
                    with eng.Fori(apart // 2, last // 2) as i:
                        for b in range(2):
                            body(i * 2 + b, b, slots, slots)
                before = slots

        def layer_1(eng, pair, quad, peel):
            for p in range(EARLY):
                pair(p, p % 2, RANGES[0][2], PAIRS + p)
            first, last = QUADS
            for q in range(first, peel):
                quad(q, q % 2, PAIRS + EARLY - first + q)
            with eng.Fori(peel // 2, (last - 3) // 2) as i:
                for b in range(2):
                    quad(i * 2 + b, b, i * 2 + (PAIRS + EARLY - first + b))
            for q in range(last - 3, last):
                quad(q, q % 2, PAIRS + EARLY - first + q)
            for p in range(LATE, PAIRS):
                at = JOBS[1] - PAIRS + p
                pair(p, at % 2, RANGES[-1][2], at)

        def quad_slots(q):
            return SLOTS if isinstance(q, int) and q < TURNED else LATER_SLOTS

        def slots_at(p, c):
            first = (p * 2 + c) * SLOTS
            return slice(first, first + SLOTS) if isinstance(p, int) else bass.ds(first, SLOTS)

        def tiles_of(p):
            return (1,) if isinstance(p, int) and p == 0 else (0, 1)

        def of_c(p, c):
            return p + c

        def groups(eng, body):
            for g in range(2):
                body(g, g)
            with eng.Fori(1, GROUPS // 2) as i:
                for b in range(2):
                    body(i * 2 + b, b)

        block = ctx.enter_context(nc.Block())

        @block.sync
        def _(sp):
            for k, (lo, hi) in enumerate(EQUAL):
                sp.dma_start(xs[:, lo * F:hi * F].rearrange("p (t f) -> p t f", f=F),
                             x[lo * P:hi * P, :].rearrange("(t p) f -> p t f", p=P)).then_inc(x_landed[k], 16)
            for half in range(2):
                sp.dma_start(w_in[0][:, half * F:(half + 1) * F], w0).then_inc(w_landed, 16)
                sp.dma_start(w_in[1][half * F:(half + 1) * F, :], w1).then_inc(w_landed, 16)
            for l, a in enumerate((a0, a1)):
                sp.dma_start(a_in[l][:, 0:1], a[F:2 * F, :]).then_inc(w_landed, 16)
                sp.dma_start(a_in[l][:, 1:2], a[0:F, :]).then_inc(w_landed, 16)
            def store_table(l):
                for k, (lo, hi) in enumerate(EQUAL):
                    sp.wait_ge(wh_copied, GROUPS * l + hi // G4)
                    sp.dma_start(tabs[l][lo * P:hi * P, :].rearrange("(t p) c -> p t c", p=P),
                                 wh[:, lo * ROW:hi * ROW].rearrange("p (t c) -> p t c", c=ROW)).then_inc(table_stored, 16)
                sp.wait_ge(mean_ready, l + 1)
                sp.dma_start(tabs[l][N:N + 1, :], mean_wh[:, :]).then_inc(table_stored, 16)
                sp.dma_start(scores_row[l].rearrange("(t p) -> t p", p=P), scores_t[:, :]).then_inc(table_stored, 16)

            def load_dense(l):
                if l == 0:
                    sp.wait_ge(signed[0], PAIRS - 1)
                else:
                    sp.wait_ge(dense_scored, l)
                sp.dma_start(ring[0][:, :], adj[0:P, :]).then_inc(dense_landed, 16)
                if l == 0:
                    sp.wait_ge(signed[1], PAIRS)
                else:
                    sp.wait_ge(y_ready, len(TILE_0_LAST))
                    store_table(1)
                sp.wait_ge(table_stored, STORES * (l + 1))
                for k in range(PARTS):
                    part = slice(k * PART, (k + 1) * PART)
                    sp.dma_start(ringf[1][:, part],
                                 scores_row[l][part].rearrange("(a n) -> a n", a=1).broadcast_to([P, PART]))\
                        .then_inc(scores_landed[k], 16)

            def load(p, b, slots, before):
                for c in tiles_of(p):
                    if past(p, 2 - c):
                        sp.wait_ge(signed[c], of_c(p, c) - 1)
                    for part in range(PARTS):
                        sp.dma_start(ring[c][:, part * PART:(part + 1) * PART],
                                     adj[tile_rows(p * 2 + c), part * PART:(part + 1) * PART]).then_inc(adj_landed[c], 16)
                    if isinstance(p, int) and p == 1 and c == 0:
                        store_table(0)

            pairs(sp, load)
            load_dense(0)
            load_dense(1)
            for k, (lo, hi, _) in enumerate(PIECES_1):
                sp.wait_ge(y_ready, len(TILE_0_LAST) + k + 1)
                sp.dma_start(out[lo * P:hi * P, :].rearrange("(t p) f -> p t f", p=P),
                             acc[:, lo * F:hi * F].rearrange("p (t f) -> p t f", f=F)).then_inc(out_stored, 16)
            sp.wait_ge(out_stored, 16 * len(PIECES_1))

        @block.gpsimd
        def _(pool):
            pool.memset(ident[:, :], 0.0).then_inc(consts0, 1)
            pool.wait_ge(consts0, 1)
            pool.affine_select(out=ident[:, :], in_=ident[:, :], compare_op=ALU.not_equal, fill=1.0,
                               base=0, pattern=[[-1, P]], channel_multiplier=1).then_inc(consts, 1)
            for l in range(2):
                pool.memset(wx[l][:, :], 0.0).then_inc(wx_zeroed, 1)
            pool.memset(tile_sum[:, :], 0.0)
            pool.wait_ge(var_ready, 1)
            pool.memset(both_G[:, :], 0.0).then_inc(zeroed, 1)
            pool.wait_ge(zeroed, 1)
            longest = pool.alloc_register("longest")
            landing = [pool.alloc_register(f"landing{b}") for b in range(2)]
            for b in range(2):
                pool.reg_mov(landing[b], 0)

            def all_in(b):
                pool.wait_ge(gathered[b], pool.snap(landing[b], min_val=16 * ALWAYS, max_val=1 << 15))
                pool.sem_inc(neighbours_in, 1)

            def some_slots(l, b, idx, first, last):
                for k in range(first, last):
                    pool.indirect_dma_start(
                        out=G[b][:, k * ROW:(k + 1) * ROW], out_offset=None, in_=tabs[l],
                        in_offset=bass.IndirectOffsetOnAxis(ap=idx[:, k:k + 1], axis=0),
                        bounds_check=MEAN_ROW, oob_is_err=False).then_inc(gathered[b], 16)
                pool.reg_add(landing[b], landing[b], 16 * (last - first))

            def gather(l, p, b, slots, at):
                if l == 0:
                    pool.wait_ge(counted, p + 1)
                if past(at, 2):
                    pool.wait_ge(weighted, at - 1)
                pool.tensor_copy(slot_idx[b][:, :], lists[:, cols(p, SLOTS)]).then_inc(idx_copied, 1)
                pool.reg_load(longest, counts[0:1, cols(p, 1)])
                most = pool.snap(longest, min_val=0, max_val=SEARCH)
                copies = at + 1 if at is p or p < EARLY else PAIRS + EARLY + p - LATE + 1
                pool.wait_ge(idx_copied, copies)
                stand_alone(pool, 1)

                some_slots(l, b, slot_idx[b], 0, ALWAYS)
                if l == 1 and past(at, PAIRS + 1):
                    all_in(1 - b)
                for first, last in zip(STEPS, STEPS[1:]):
                    if last <= slots:
                        with pool.If(most > first):
                            some_slots(l, b, slot_idx[b], first, last)
                        with pool.Else():
                            pool.nop()
                if l == 0:
                    all_in(b)

            def gather_quad(q, b, at):
                pool.wait_ge(quad_counted, q - (QUADS[0] - 1))
                pool.wait_ge(weighted, at - 1)
                stand_alone(pool, 1)
                pool.reg_load(longest, quad_counts[0:1, cols(q, 1)])
                most = pool.snap(longest, min_val=0, max_val=4 * FOUND)
                some_slots(1, b, quad_idx[b], 0, QUAD_FIRST)
                all_in(1 - b)
                some_slots(1, b, quad_idx[b], QUAD_FIRST, QUAD_ALWAYS)
                for first, last in zip(QUAD_STEPS, QUAD_STEPS[1:]):
                    with pool.If(most > first):
                        some_slots(1, b, quad_idx[b], first, last)
                    with pool.Else():
                        pool.nop()

            def add_tiles(l):
                if l:
                    pool.wait_ge(mean_ready, l)
                    pool.memset(tile_sum[:, :], 0.0)

                def group(g, b):
                    pool.drain()
                    pool.wait_ge(wh_copied, GROUPS * l + g + 1)
                    pool.tensor_tensor(tile_sum[:, :], tile_sum[:, :], wh[:, cols(g, G4 * ROW)], ALU.add)

                groups(pool, group)
                pool.drain().then_inc(tiles_added, 1)

            add_tiles(0)
            pool.wait_ge(table_stored, STORES)
            pairs(pool, lambda p, b, slots, before: gather(0, p, b, slots, p))
            add_tiles(1)
            pool.wait_ge(table_stored, STORES * 2)
            layer_1(pool, lambda p, b, slots, at: gather(1, p, b, slots, at), gather_quad, QUADS[0])
            all_in((JOBS[1] - 1) % 2)

        @block.scalar
        def _(act):
            act.wait_ge(w_turned, 2)
            act.activation(w_t[0][:, :], psT[0][0:2 * F, 0:F], ACT.Copy).then_inc(wt_copied, 1)
            act.activation(w_t[1][:, :], psT[1][0:F, 0:2 * F], ACT.Copy).then_inc(wt_copied, 1)
            act.wait_ge(a_through, 2)
            act.wait_ge(wt_copied, 2)
            act.wait_ge(w_landed, 128)
            act.wait_ge(wx_zeroed, 2)
            for l, w in enumerate((w_t[0], w_in[1])):
                for half in range(2):
                    rows, at = slice(half * F, (half + 1) * F), half * ROW
                    act.activation(wx[l][rows, at:at + F], w[rows, :], ACT.Copy).then_inc(wx_ready, 1)
                    act.activation(wx[l][rows, at + F:at + ROW], psW[l][rows, 0:2], ACT.Copy).then_inc(wx_ready, 1)

            def square(l, k):
                lo, hi = (EQUAL, TILE_0_LAST)[l][k]
                act.wait_ge(centred, l * CHUNKS + k + 1)
                act.activation(scratch[:, lo * F:hi * F], acc[:, lo * F:hi * F], ACT.Square).then_inc(squared, 1)

            def features(l):
                act.wait_ge(var_ready, l + 1)
                act.activation(std[:, :], var[:, :], ACT.Sqrt).then_inc(std_ready, 1)

                def copy_rows(g, b):
                    act.wait_ge(wh_done, GROUPS * l + g + 1)
                    act.activation(wh[:, cols(g, G4 * ROW)], psW[b][:, 0:G4 * ROW], ACT.Copy).then_inc(wh_copied, 1)

                def group(g, b):
                    at = GROUPS * l + g
                    act.wait_ge(h_turned, at + 1)
                    if past(at, 2):
                        act.wait_ge(wh_done, at - 1)
                    act.activation(hT[b][:, :], psT[b][:, 0:G4 // 2 * P], ACT.Copy).then_inc(hT_ready, 1)
                    if past(g, 1):
                        copy_rows(g - 1, 1 - b)

                groups(act, group)
                copy_rows(GROUPS - 1, 1)

            def dense_own(l):
                for k in range(PARTS):
                    part = slice(k * PART, (k + 1) * PART)
                    act.wait_ge(scores_landed[k], 16 * (l + 1))
                    act.activation(ringf[1][:, part], ringf[1][:, part], ACT.Identity, bias=wh[:, OWN_COL:ROW])\
                        .then_inc(dense_added, 1)

            def dense_exp(l, parts=range(PARTS)):
                act.wait_ge(dense_scored, l + 1)
                for k in parts:
                    part = slice(k * PART, (k + 1) * PART)
                    act.activation(ringf[1][:, part], ringf[1][:, part], ACT.Exp, bias=dense_neg[:, :],
                                   accum_out=dense_sums[:, k:k + 1]).then_inc(dense_exped, 1)

            def dense_turn(l, first=0, last=GROUPS):
                for q in range(first, last):
                    at = GROUPS * l + q
                    act.wait_ge(p_turned, at + 1)
                    if past(at, 2):
                        act.wait_ge(dense_block, at - 1)
                    act.activation(pT[q % 2][:, :], psT[q % 2][:, :], ACT.Copy).then_inc(pT_ready, 1)
                if last < GROUPS:
                    return
                act.wait_ge(dense_block, GROUPS * (l + 1))
                act.activation(dense_acc[:, :], psW[0][:, 0:F], ACT.Copy).then_inc(dense_copied, 1)

            def exp(at, b, width):
                act.wait_ge(scored, at + 1)
                act.activation(pexp[b][:, 0:width], e[b][:, 0:width], ACT.Exp).then_inc(exped, 1)

            def copy_sum(at, b, p, tiles=2):
                act.wait_ge(summed, at + 1)
                act.activation(acc[:, cols(p, tiles * F)], psS[b][:, 0:tiles * F], ACT.Copy).then_inc(acc_copied, 1)

            def sign(p, b):
                for c in tiles_of(p):
                    act.wait_ge(adj_landed[c], of_c(p, c) * (16 * PARTS))
                    if past(p, 2 - c):
                        act.wait_ge(searched[c], of_c(p, c) - 1)
                    for s in range(NSEG):
                        lo, hi = SEGS[s], SEGS[s + 1]
                        done = act.activation(signs[c][:, lo + 8 * s:hi + 8 * s], ring[c][:, lo:hi], ACT.Sign)
                        if s == 2 and c == 0 and past(p, 3):
                            exp(p - 3, 1 - b, 2 * SLOTS)
                    done.then_inc(signed[c], 1)
                if past(p, 4):
                    copy_sum(p - 4, b, p - 4)

            def general(l):
                act.wait_ge(g_used[l], 1)
                with act.Fori(0, F) as f:
                    act.dma_start(wh_cols[l][bass.ds(f, 1), :],
                                  tabs[l][0:N, bass.ds(f, 1)].rearrange("n a -> a n"),
                                  allow_slow_non_contiguous=True).then_inc(g_column[l], 16)
                    act.wait_ge(g_column[l], f * 16 + 16)
                with act.Fori(0, TILES) as t:
                    act.wait_ge(g_used[l], t * (F + 1) + 1)
                    act.dma_start(ring[0][:, :], adj[bass.ds(t * P, P), :]).then_inc(g_landed[l], 16)
                    act.dma_start(ringf[1], scores_row[l].rearrange("(a n) -> a n", a=1).broadcast_to([P, N]))\
                        .then_inc(g_landed[l], 16)
                    act.wait_ge(g_landed[l], t * 32 + 32)
                    act.activation(ringf[1], ringf[1], ACT.Identity,
                                   bias=wh[:, bass.ds(t * ROW + OWN_COL, 1)]).then_inc(g_added[l], 1)
                    act.wait_ge(g_scored[l], t + 1)
                    act.activation(ringf[1], ringf[1], ACT.Exp, bias=dense_neg[:, :],
                                   accum_out=dense_sum[:, :]).then_inc(g_exped[l], 1)
                    with act.Fori(0, F) as f:
                        act.wait_ge(g_used[l], t * (F + 1) + f + 1)
                        act.dma_start(feature[:, :], wh_cols[l][bass.ds(f, 1), :].broadcast_to([P, N]))\
                            .then_inc(g_feature[l], 16)

            def elu(part, room, at):
                act.wait_ge(scaled, at)
                act.activation(room, acc[:, part], ACT.Relu, scale=-1.0).then_inc(neg_ready, 1)
                act.wait_ge(neg_ready, at)
                act.activation(room, room, ACT.Exp, scale=-1.0).then_inc(elu_exped, 1)

            def elu_0(k):
                lo, hi = TILE_0_LAST[k]
                elu(slice(lo * F, hi * F), scratch[:, lo * F:hi * F], k + 1)

            def elu_1(k):
                lo, hi, _ = PIECES_1[k]
                elu(slice(lo * F, hi * F), scratch_1[k % 2][:, 0:(hi - lo) * F], len(TILE_0_LAST) + k + 1)

            for k in range(CHUNKS):
                square(0, k)
            features(0)
            act.wait_ge(sentinels_set, 1)
            sign(0, 0)
            for p in range(1, 4):
                sign(p, p % 2)
            with act.Fori(2, PAIRS // 2) as i:
                for b in range(2):
                    sign(i * 2 + b, b)
            exp(PAIRS - 3, 1, 2 * SLOTS)
            copy_sum(PAIRS - 4, 0, PAIRS - 4)
            copy_sum(PAIRS - 3, 1, PAIRS - 3)
            dense_own(0)
            exp(PAIRS - 2, 0, 2 * SLOTS)
            copy_sum(PAIRS - 2, 0, PAIRS - 2)

            def finish_layer_0(turning):
                if turning:
                    dense_exp(0, (0,))
                    exp(PAIRS - 1, 1, 2 * SLOTS)
                    dense_exp(0, (1, 2, 3))
                elu_0(0)
                if turning:
                    dense_turn(0, 0, 2)
                    copy_sum(PAIRS - 1, 1, PAIRS - 1)
                elu_0(1)
                for q in range(2, GROUPS):
                    if turning:
                        dense_turn(0, q, q + 1)
                    if q in (3, 6):
                        elu_0(1 + q // 3)
                    if q in (5, 8, 11):
                        square(1, q // 3 - 1)
                square(1, 3)
                elu_0(4)
                square(1, 4)

            def with_general(l, few, many):
                reg = act.alloc_register(f"act_flag{l}")
                act.wait_ge(flag_ready, l + 1)
                act.reg_load(reg, flag[0:1, 0:1])
                some = act.snap(reg, min_val=0, max_val=N)
                with act.If(some > 0):
                    many()
                with act.Else():
                    few()

            def general_0():
                dense_exp(0)
                exp(PAIRS - 1, 1, 2 * SLOTS)
                dense_turn(0, 0, 2)
                copy_sum(PAIRS - 1, 1, PAIRS - 1)
                dense_turn(0, 2)
                act.wait_ge(dense_landed, 32)
                general(0)
                act.wait_ge(g_used[0], TILES * (F + 1) + 1)
                act.dma_start(ring[0][:, :], adj[0:P, :]).then_inc(g_landed[0], 16)
                act.wait_ge(g_landed[0], TILES * 32 + 16)
                finish_layer_0(False)

            with_general(0, lambda: finish_layer_0(True), general_0)
            features(1)

            def copy_before(at, b, p=None, q=None):
                if q is not None and past(q, QUADS[0] + 1):
                    copy_sum(at - 1, 1 - b, q - 1, 4)
                elif q is not None:
                    copy_sum(at - 1, 1 - b, EARLY - 1)
                elif p == LATE:
                    copy_sum(at - 1, 1 - b, QUADS[1] - 1, 4)
                elif p > 0:
                    copy_sum(at - 1, 1 - b, p - 1)

            def pair(p, b, slots, at):
                if p == PAIRS - 1:
                    elu_1(4)
                exp(at, b, 2 * slots)
                copy_before(at, b, p=p)
                if p == 1:
                    dense_own(1)
                if p == 3:
                    dense_exp(1)

            def quad(q, b, at):
                exp(at, b, 4 * quad_slots(q))
                if isinstance(q, int) and q < TURNED:
                    dense_turn(1, (q - QUADS[0]) * 4, (q - QUADS[0] + 1) * 4)
                copy_before(at, b, q=q)
                if isinstance(q, int) and q in ELU_AT:
                    elu_1(ELU_AT[q])

            layer_1(act, pair, quad, APART)
            copy_sum(JOBS[1] - 1, (JOBS[1] - 1) % 2, PAIRS - 1)
            elu_1(5)

            def general_1():
                act.wait_ge(out_stored, 16 * len(PIECES_1))
                general(1)
                elu(slice(0, TILES * F), scratch_g, G_PIECE)
                act.wait_ge(y_ready, G_PIECE)
                act.dma_start(out.rearrange("(t p) f -> p t f", p=P),
                              acc[:, :].rearrange("p (t f) -> p t f", f=F)).then_inc(out_stored, 16)
                act.wait_ge(out_stored, 16 * len(PIECES_1) + 16)

            with_general(1, act.nop, general_1)

        @block.tensor
        def _(pe):
            pe.wait_ge(consts, 1)
            pe.wait_ge(sentinels_set, 1)
            pe.wait_ge(w_landed, 128)
            pe.transpose(psT[0][0:2 * F, 0:F], w_in[0][:, :], ident[0:F, 0:F]).then_inc(w_turned, 1)
            pe.transpose(psT[1][0:F, 0:2 * F], w_in[1][:, :], ident[:, :]).then_inc(w_turned, 1)
            pe.matmul(psW[0][0:2 * F, 0:2], w_in[0][:, :], a_in[0][:, :], start=True, stop=True).then_inc(a_through, 1)
            pe.wait_ge(wt_copied, 2)
            pe.matmul(psW[1][0:2 * F, 0:2], w_t[1][:, :], a_in[1][:, :], start=True, stop=True).then_inc(a_through, 1)
            pe.wait_ge(wx_ready, 8)

            def features(l):
                def multiply(g, b):
                    at = GROUPS * l + g
                    pe.wait_ge(hT_ready, at + 1)
                    if past(at, 2):
                        pe.wait_ge(wh_copied, at - 1)
                    for k in range(G4 // 2):
                        done = pe.matmul(psW[b][:, k * 2 * ROW:(k + 1) * 2 * ROW], hT[b][:, k * P:(k + 1) * P],
                                         wx[l][:, :], start=True, stop=True)
                    done.then_inc(wh_done, 1)

                def group(g, b):
                    at = GROUPS * l + g
                    pe.wait_ge(h_ready, at + 1)
                    if past(at, 2):
                        pe.wait_ge(hT_ready, at - 1)
                        stand_alone(pe, 0)
                    for k in range(G4 // 2):
                        done = pe.transpose(psT[b][:, k * P:(k + 1) * P], hst[b][:, k * 2 * F:(k + 1) * 2 * F], ident[:, :])
                    done.then_inc(h_turned, 1)
                    if past(g, 1):
                        multiply(g - 1, 1 - b)

                groups(pe, group)
                multiply(GROUPS - 1, 1)
                pe.wait_ge(wh_copied, GROUPS * (l + 1))
                if l:
                    pe.wait_ge(flag_ready, l)
                scores = wh[:, :].rearrange("p (t c) -> p t c", c=ROW)[:, :, SCORE_COL]
                pe.matmul(psD[0][0:TILES, 0:P], scores, ident[:, :], start=True, stop=True)
                pe.wait_ge(tiles_added, l + 1)
                pe.matmul(psD[1][0:1, 0:G4 * ROW], over_n[:, :], tile_sum[:, :], start=True, stop=True)\
                    .then_inc(mean_summed, 1)

            def dense(l, first=0, last=GROUPS + 1):
                if first == 0:
                    pe.wait_ge(wh_copied, GROUPS * (l + 1))
                for q in range(first, last):
                    if q < GROUPS:
                        if q % (GROUPS // PARTS) == 0:
                            pe.wait_ge(dense_exped, PARTS * l + q * PARTS // GROUPS + 1)
                        if past(GROUPS * l + q, 2):
                            pe.wait_ge(pT_ready, GROUPS * l + q - 1)
                        for k in range(G4):
                            j = q * G4 + k
                            done = pe.transpose(psT[q % 2][:, k * P:(k + 1) * P], ringf[1][:, j * P:(j + 1) * P], ident[:, :])
                        done.then_inc(p_turned, 1)
                    if q > 0:
                        pe.wait_ge(pT_ready, GROUPS * l + q)
                        for k in range(G4):
                            j = (q - 1) * G4 + k
                            done = pe.matmul(psW[0][:, 0:F], pT[(q - 1) % 2][:, k * P:(k + 1) * P],
                                             wh[:, j * ROW:j * ROW + F], start=(j == 0), stop=(j == TILES - 1))
                        done.then_inc(dense_block, 1)

            def turn_lengths(p, b):
                pe.wait_ge(listed, p + 1)
                if past(p, 2):
                    pe.wait_ge(counted, p - 1)
                pe.matmul(psD[b][0:1, 0:P], length[b][:, :], ident[:, :], start=True, stop=True)\
                    .then_inc(lengths_turned, 1)

            def sum_slots(at, b, slots, terms, tiles=2):
                pe.wait_ge(weighted, at + 1)
                if past(at, 2):
                    pe.wait_ge(acc_copied, at - 1)
                for k in range(slots):
                    done = pe.matmul(psS[b][:, 0:tiles * F], ident[:, :], terms[:, k * tiles * F:(k + 1) * tiles * F],
                                     start=(k == 0), stop=(k == slots - 1))
                done.then_inc(summed, 1)

            def turn_over(l):
                pe.wait_ge(over_ready, l + 1)
                pe.matmul(psD[0][0:1, 0:P], over[:, :], ident[:, :], start=True, stop=True).then_inc(over_turned, 1)

            def first(p, b, slots, before):
                turn_lengths(p, b)
                if past(p, 2):
                    sum_slots(p - 2, b, before, prod)

            features(0)
            pe.wait_ge(mean_ready, 1)
            pairs(pe, first, lag=2)
            turn_over(0)
            sum_slots(PAIRS - 2, 0, RANGES[-1][2], prod)

            def warm(products):
                for _ in range(products):
                    pe.matmul(psT[0][:, 0:P], ident[:, :], ident[:, :], start=True, stop=True)

            warm(2 * WARMING)
            dense(0, 0, 2)
            sum_slots(PAIRS - 1, 1, RANGES[-1][2], prod)
            dense(0, 2)
            pe.wait_ge(dense_copied, 1)
            warm(WARMING)
            features(1)

            def turn_quad_lengths(q, b):
                pe.wait_ge(quad_listed, q - (QUADS[0] - 1))
                if past(q, QUADS[0] + 2):
                    pe.wait_ge(quad_counted, q - (QUADS[0] + 1))
                pe.matmul(psD[b][0:1, 0:P], length[b][:, :], ident[:, :], start=True, stop=True)\
                    .then_inc(quad_lengths_turned, 1)

            def quad(q, b, at):
                if not isinstance(q, int) or q < QUADS[1] - 2:
                    turn_quad_lengths(q + 2, b)
                if isinstance(q, int) and q < TURNED:
                    dense(1, (q - QUADS[0]) * 4, (q - QUADS[0] + 1) * 4 if q < TURNED - 1 else GROUPS + 1)
                sum_slots(at, b, quad_slots(q), quad_prod[b], 4)
                if isinstance(q, int) and q == QUADS[1] - 2:
                    turn_over(1)

            pe.wait_ge(mean_ready, 2)
            for q in range(QUADS[0], QUADS[0] + 2):
                turn_quad_lengths(q, q % 2)
            def pair(p, b, slots, at):
                if p == PAIRS - 1:
                    warm(WARMING // 3)
                sum_slots(at, b, slots, prod)

            layer_1(pe, pair, quad, APART)

        @block.vector
        def _(dve):
            dve.memset(ones8[:, :], 1.0)
            dve.memset(over_n[:, :], 1.0 / N)
            for c in range(2):
                for s in range(NSEG):
                    at = c * FOUND + 8 * s
                    dve.memset(seg_base[:, at:at + 8], float(c * KEYS + SEGS[s] + 1))
                    dve.memset(seg_len[:, at:at + 8], float(SEGS[s + 1] - SEGS[s]))
                    end = SEGS[s + 1] + 8 * s
                    dve.memset(signs[c][:, end:end + 8], 1.0)
                dve.memset(mean_key[:, c:c + 1], float(c * KEYS + MEAN_ROW + 1))
            dve.memset(found[:, :], N)
            for c in range(5):
                dve.memset(limits[:, c * SLOTS:(c + 1) * SLOTS], float(c * KEYS))
            dve.memset(over[:, :], 0.0).then_inc(sentinels_set, 1)

            def piece(v, lo, hi):
                w = v.shape[1] // TILES
                return v[:, lo * w:hi * w].rearrange("p (t f) -> p t f", f=w)

            def over_features(v, lo, hi):
                return v[:, lo:hi].rearrange("p (t a) -> p t a", a=1).broadcast_to([P, hi - lo, F])

            def centre(lo, hi):
                dve.tensor_reduce(row_sum[:, lo:hi], piece(xs, lo, hi), AX.X, ALU.add)
                dve.drain()
                dve.scalar_tensor_tensor(piece(acc, lo, hi), over_features(row_sum, lo, hi), -1.0 / F,
                                         piece(xs, lo, hi), ALU.mult, ALU.add).then_inc(centred, 1)

            def sum_squares(n, lo, hi):
                dve.wait_ge(squared, n)
                dve.tensor_reduce(var[:, lo:hi], piece(scratch, lo, hi), AX.X, ALU.add)

            def features(l):
                dve.drain()
                dve.tensor_scalar(var[:, :], var[:, :], 1.0 / F, EPS, ALU.mult, ALU.add).then_inc(var_ready, 1)
                dve.wait_ge(std_ready, l + 1)
                dve.reciprocal(rstd[:, :], std[:, :])
                dve.drain()

                def group(g, b):
                    if past(GROUPS * l + g, 2):
                        dve.wait_ge(h_turned, GROUPS * l + g - 1)
                    r = rstd[:, cols(g, G4)].rearrange("p (t a) -> p t a", a=1).broadcast_to([P, G4, F])
                    dve.scalar_tensor_tensor(hst[b][:, :].rearrange("p (t f) -> p t f", f=F),
                                             acc[:, cols(g, G4 * F)].rearrange("p (t f) -> p t f", f=F),
                                             0.0, r, ALU.max, ALU.mult).then_inc(h_ready, 1)

                groups(dve, group)

            def finish_table(l):
                dve.wait_ge(mean_summed, l + 1)
                dve.tensor_copy(scores_t[:, :], psD[0][0:TILES, 0:P])
                dve.drain()
                dve.tensor_reduce(mean_wh[:, :], psD[1][0:1, 0:G4 * ROW].rearrange("p (k c) -> p c k", c=ROW),
                                  AX.X, ALU.add).then_inc(mean_ready, 1)

            def dense_scores(added, count, steps=(0, 1, 2), parts=1):
                if 0 in steps:
                    dve.tensor_scalar(ringf[0], ring[0][:, :], 0, NEG, ALU.is_le, ALU.mult)
                    dve.drain()
                if 1 in steps:
                    for k in range(parts):
                        part = slice(k * (N // parts), (k + 1) * (N // parts))
                        dve.wait_ge(added, count + k)
                        dve.scalar_tensor_tensor(ringf[1][:, part], ringf[1][:, part], ALPHA, ringf[1][:, part],
                                                 ALU.mult, ALU.max)
                    dve.drain()
                if 2 in steps:
                    dve.tensor_tensor_reduce(ringf[1], ringf[1], ringf[0], 1.0, NEG, ALU.add, ALU.max, dense_max[:, :])
                    dve.drain()
                    return dve.tensor_scalar(dense_neg[:, :], dense_max[:, :], -1.0, None, ALU.mult)

            def dense(l, steps):
                if 0 in steps:
                    dve.wait_ge(dense_landed, 16 * (l + 1))
                done = dense_scores(dense_added, PARTS * l + 1, steps, PARTS)
                if 2 in steps:
                    done.then_inc(dense_scored, 1)

            def search(c):
                for s in range(NSEG):
                    at = c * FOUND + 8 * s
                    done = dve.max_index(found[:, at:at + 8], ones8[:, :],
                                         signs[c][:, SEGS[s] + 8 * s:SEGS[s + 1] + 8 * s + 8])
                done.then_inc(searched[c], 1)

            def by_tile(v, slots, tiles=2):
                return v[:, 0:tiles * slots].rearrange("p (c k) -> p c k", c=tiles)

            def make_lists(p, b, slots):
                dve.drain()
                dve.tensor_tensor(place[:, :], found[:, :], seg_base[:, :], ALU.add)
                dve.tensor_tensor(valid[:, :], found[:, :], seg_len[:, :], ALU.is_lt)
                dve.drain()
                dve.tensor_tensor(key[0][:, 0:SEARCH], place[:, :], valid[:, :], ALU.mult)
                dve.tensor_reduce(degree[:, :], valid[:, :].rearrange("p (c k) -> p c k", c=2), AX.X, ALU.add)
                dve.tensor_reduce(last_key[:, :], valid[:, 7:SEARCH:8], AX.X, ALU.max)
                dve.drain()
                dve.scalar_tensor_tensor(key[0][:, SEARCH:SEARCH + 2], degree[:, :], 0.0, mean_key[:, :],
                                         ALU.is_equal, ALU.mult)
                dve.tensor_scalar(entries[:, :], degree[:, :], 1.0, None, ALU.max)
                dve.tensor_tensor(over[:, :], over[:, :], last_key[:, :], ALU.max)
                dve.drain()
                dve.tensor_tensor(length[b][:, :], entries[:, 0:1], entries[:, 1:2], ALU.add)
                for r in range(0, SLOTS, 8):
                    this, other = key[r // 8 % 2], key[1 - r // 8 % 2]
                    if r >= slots:
                        dve.memset(top[:, r:r + 8], 0.0)
                        continue
                    dve.max(top[:, r:r + 8], this[:, :])
                    dve.drain()
                    if r == 0:
                        dve.scalar_tensor_tensor(over[:, :], length[b][:, :], float(-slots), over[:, :],
                                                 ALU.add, ALU.max)
                    if r + 8 < slots:
                        dve.match_replace(other[:, :], top[:, r:r + 8], this[:, :], 0.0)
                        dve.drain()
                dve.drain()
                pen_first, pen_second = (pens[:, slots_at(p, c)] for c in range(2))
                dve.tensor_scalar(gap[:, :], top[:, :], 0.0, float(SKIP), ALU.is_equal, ALU.mult)
                dve.tensor_scalar(of_second[:, :], top[:, :], float(KEYS), float(-KEYS), ALU.is_gt, ALU.mult)
                dve.tensor_scalar(pen_second, top[:, :], float(KEYS), NEG, ALU.is_le, ALU.mult)
                dve.drain()
                dve.tensor_tensor(shift[:, :], gap[:, :], of_second[:, :], ALU.add)
                dve.drain()
                dve.tensor_scalar(pen_first, shift[:, :], 0.0, NEG, ALU.not_equal, ALU.mult)
                dve.scalar_tensor_tensor(lists[:, cols(p, SLOTS)], top[:, :], -1.0, shift[:, :], ALU.add, ALU.add)\
                    .then_inc(listed, 1)

            def count(p, b):
                dve.wait_ge(lengths_turned, p + 1)
                dve.tensor_reduce(counts[0:1, cols(p, 1)], psD[b][0:1, 0:P], AX.X, ALU.max).then_inc(counted, 1)

            def make_quad(q, b, slots):
                idx = by_tile(lists[:, cols(q, 2 * SLOTS)], SLOTS)
                pen_second = pens[:, cols(q, 4 * SLOTS)].rearrange("p (j c k) -> p j c k", j=2, c=2)[:, :, 1]
                dve.tensor_scalar(by_tile(second_rows, SLOTS), pen_second, 0.0, float(KEYS), ALU.is_equal, ALU.mult)
                dve.drain()
                for j in range(2):
                    part = slice(j * SLOTS, (j + 1) * SLOTS)
                    dve.scalar_tensor_tensor(quad_key[1][:, part], idx[:, j], float(1 + 2 * j * KEYS),
                                             second_rows[:, part], ALU.add, ALU.add)
                dve.drain()
                dve.scalar_tensor_tensor(by_tile(quad_key[0], SLOTS), idx, float(SKIP - 1), by_tile(quad_key[1], SLOTS),
                                         ALU.is_lt, ALU.mult)
                dve.drain()
                dve.tensor_scalar(second_rows[:, :], quad_key[0][:, :], 0.0, None, ALU.is_gt)
                dve.drain()
                dve.tensor_reduce(length[b][:, :], second_rows[:, :], AX.X, ALU.add)
                for r in range(0, SLOTS, 8):
                    this, other = quad_key[r // 8 % 2], quad_key[1 - r // 8 % 2]
                    dve.max(quad_top[:, r:r + 8], this[:, :])
                    dve.drain()
                    if r + 8 < SLOTS:
                        dve.match_replace(other[:, :], quad_top[:, r:r + 8], this[:, :], 0.0)
                        dve.drain()
                dve.scalar_tensor_tensor(over[:, :], length[b][:, :], float(-slots), over[:, :], ALU.add, ALU.max)
                dve.tensor_tensor(by_tile(beyond, SLOTS, 5),
                                  quad_top[:, :].rearrange("p (a k) -> p a k", a=1).broadcast_to([P, 5, SLOTS]),
                                  by_tile(limits, SLOTS, 5), ALU.is_gt)
                dve.tensor_scalar(gap[:, :], quad_top[:, :], 0.0, float(SKIP), ALU.is_equal, ALU.mult)
                dve.drain()
                dve.tensor_tensor(z[:, :], beyond[:, SLOTS:5 * SLOTS], beyond[:, 0:4 * SLOTS], ALU.subtract)
                dve.tensor_tensor(shift[:, :], beyond[:, SLOTS:2 * SLOTS], beyond[:, 2 * SLOTS:3 * SLOTS], ALU.add)
                dve.scalar_tensor_tensor(gap[:, :], beyond[:, 3 * SLOTS:4 * SLOTS], float(-KEYS), gap[:, :],
                                         ALU.mult, ALU.add)
                dve.drain()
                dve.tensor_scalar(quad_pens[b][:, :], z[:, :], 1.0, NEG, ALU.add, ALU.mult)
                dve.scalar_tensor_tensor(shift[:, :], shift[:, :], float(-KEYS), gap[:, :], ALU.mult, ALU.add)
                dve.drain()
                dve.scalar_tensor_tensor(quad_idx[b][:, :], quad_top[:, :], -1.0, shift[:, :], ALU.add, ALU.add)\
                    .then_inc(quad_listed, 1)

            def count_quad(q, b):
                dve.wait_ge(quad_lengths_turned, q - (QUADS[0] - 1))
                dve.tensor_reduce(quad_counts[0:1, cols(q, 1)], psD[b][0:1, 0:P], AX.X, ALU.max)\
                    .then_inc(quad_counted, 1)

            def score(at, p, b, slots, pen, tiles=2):
                dve.wait_ge(neighbours_in, at + 1)
                scores = G[b][:, 0:slots * ROW].rearrange("p (a k r) -> p a k r", a=1, r=ROW)[:, :, :, SCORE_COL]
                own = wh[:, cols(p, tiles * ROW)].rearrange("p (c r) -> p c r", c=tiles)[:, :, OWN_COL:ROW]
                zs = by_tile(z, slots, tiles)
                dve.tensor_tensor(zs, scores.broadcast_to([P, tiles, slots]), own.broadcast_to([P, tiles, slots]), ALU.add)
                dve.drain()
                dve.scalar_tensor_tensor(zs, zs, ALPHA, zs, ALU.mult, ALU.max)
                dve.drain()
                dve.tensor_tensor(zs, zs, pen, ALU.add)
                dve.drain()
                dve.tensor_reduce(rowmax[:, 0:tiles], zs, AX.X, ALU.max)
                dve.drain()
                dve.tensor_tensor(by_tile(e[b], slots, tiles), zs,
                                  rowmax[:, 0:tiles].rearrange("p (c a) -> p c a", a=1).broadcast_to([P, tiles, slots]),
                                  ALU.subtract).then_inc(scored, 1)

            def pair_pens(p, slots):
                return pens[:, cols(p, 2 * SLOTS)].rearrange("p (c k) -> p c k", c=2)[:, :, 0:slots]

            def weigh(at, p, b, slots, terms, tiles=2):
                dve.wait_ge(exped, at + 1)
                if past(at, 1):
                    dve.wait_ge(summed, at + 1 - tiles // 2)
                rows = G[b][:, 0:slots * ROW].rearrange("p (k r) -> p k r", r=ROW)[:, :, 0:F]
                for c in range(tiles):
                    w = pexp[b][:, c * slots:(c + 1) * slots].rearrange("p (k a) -> p k a", a=1)
                    done = dve.tensor_tensor(terms[:, 0:slots * tiles * F].rearrange("p (k c f) -> p c k f", c=tiles, f=F)[:, c],
                                             rows, w.broadcast_to([P, slots, F]), ALU.mult)
                done.then_inc(weighted, 1)
                dve.tensor_reduce(sums[:, cols(p, tiles)], by_tile(pexp[b], slots, tiles), AX.X, ALU.add)

            def stream(p, b, slots, before):
                for c in tiles_of(p):
                    dve.wait_ge(signed[c], of_c(p, c))
                    stand_alone(dve, 2)
                    search(c)
                    if c == 0 and past(p, 2):
                        score(p - 2, p - 2, b, before, pair_pens(p - 2, before))
                make_lists(p, b, slots)
                if past(p, 2):
                    weigh(p - 2, p - 2, b, before, prod)
                count(p, b)

            def general(l, then=None):
                reg = dve.alloc_register(f"dve_flag{l}")
                dve.wait_ge(flag_ready, l + 1)
                dve.drain()
                dve.reg_load(reg, flag[0:1, 0:1])
                some = dve.snap(reg, min_val=0, max_val=N)
                dve.drain().then_inc(g_used[l], 1)
                with dve.If(some > 0):
                    dve.wait_ge(acc_copied, JOBS[l])
                    with dve.Fori(0, TILES) as t:
                        dve.wait_ge(g_landed[l], t * 32 + 32)
                        dense_scores(g_added[l], t + 1).then_inc(g_scored[l], 1)
                        dve.wait_ge(g_exped[l], t + 1)
                        dve.tensor_copy(sums[:, bass.ds(t, 1)], dense_sum[:, :])
                        with dve.Fori(0, F) as f:
                            dve.wait_ge(g_feature[l], (t * F + f) * 16 + 16)
                            dve.scalar_tensor_tensor(ringf[0], ringf[1], 1.0, feature[:, :], ALU.mult, ALU.mult,
                                                     accum_out=acc[:, bass.ds(t * F + f, 1)]).then_inc(g_used[l], 1)
                            dve.drain()
                        dve.drain().then_inc(g_used[l], 1)
                    if then:
                        then()
                with dve.Else():
                    dve.nop()
                dve.drain()

            def scale(lo, hi):
                dve.tensor_tensor(piece(acc, lo, hi), piece(acc, lo, hi), over_features(rsums, lo, hi), ALU.mult)\
                    .then_inc(scaled, 1)

            def scale_tile_0(l):
                dve.wait_ge(dense_copied, l + 1)
                dve.tensor_reduce(sums[:, 0:1], dense_sums[:, :], AX.X, ALU.add)
                dve.drain()
                dve.reciprocal(rsums[:, 0:1], sums[:, 0:1])
                dve.drain()
                dve.tensor_tensor(acc[:, 0:F], dense_acc[:, :], rsums[:, 0:1].broadcast_to([P, F]), ALU.mult)\
                    .then_inc(scaled, 1)

            def add(lo, hi, room, y, at):
                part = slice(lo * F, hi * F)
                dve.wait_ge(elu_exped, at)
                dve.scalar_tensor_tensor(acc[:, part], room, -1.0, acc[:, part], ALU.add, ALU.max)
                dve.drain()
                dve.tensor_tensor(y[:, part], xs[:, part], acc[:, part], ALU.add).then_inc(y_ready, 1)

            def add_0(k):
                lo, hi = TILE_0_LAST[k]
                add(lo, hi, scratch[:, lo * F:hi * F], xs, k + 1)
                dve.drain()
                centre(*TILE_0_LAST[k])

            def scale_1(k):
                lo, hi, job = PIECES_1[k]
                if job is None:
                    scale_tile_0(1)
                else:
                    dve.wait_ge(acc_copied, job + 1)
                    dve.drain()
                    dve.reciprocal(rsums[:, lo:hi], sums[:, lo:hi])
                    dve.drain()
                    scale(lo, hi)

            def add_1(k):
                lo, hi, _ = PIECES_1[k]
                add(lo, hi, scratch_1[k % 2][:, 0:(hi - lo) * F], acc, len(TILE_0_LAST) + k + 1)

            def whole_residual():
                dve.drain()
                dve.reciprocal(rsums[:, :], sums[:, :])
                dve.drain()
                scale(0, TILES)
                add(0, TILES, scratch_g, acc, G_PIECE)

            def invert_sums():
                dve.drain()
                general(0)
                dve.reciprocal(rsums[:, :], sums[:, :])
                dve.drain()

            for k in range(CHUNKS + 1):
                if k < CHUNKS:
                    dve.wait_ge(x_landed[k], 16)
                    centre(*EQUAL[k])
                if k:
                    sum_squares(k, *EQUAL[k - 1])
            features(0)
            finish_table(0)
            pairs(dve, stream, lag=2)
            def set_flag(l):
                dve.wait_ge(over_turned, l + 1)
                dve.tensor_reduce(flag[:, :], psD[0][0:1, 0:P], AX.X, ALU.max).then_inc(flag_ready, 1)

            dve.drain().then_inc(over_ready, 1)
            dense(0, (0, 1))
            few = RANGES[-1][2]
            score(PAIRS - 2, PAIRS - 2, 0, few, pair_pens(PAIRS - 2, few))
            weigh(PAIRS - 2, PAIRS - 2, 0, few, prod)
            set_flag(0)
            dense(0, (2,))
            score(PAIRS - 1, PAIRS - 1, 1, few, pair_pens(PAIRS - 1, few))
            weigh(PAIRS - 1, PAIRS - 1, 1, few, prod)

            invert_sums()
            for k in range(7):
                if k < 4:
                    dve.wait_ge(acc_copied, TILE_0_LAST[k][1] // 2)
                    scale(*TILE_0_LAST[k])
                if 2 <= k < 6:
                    add_0(k - 2)
                if 3 <= k:
                    sum_squares(CHUNKS + k - 2, *TILE_0_LAST[k - 3])
                if k == 5:
                    scale_tile_0(0)
            add_0(4)
            sum_squares(CHUNKS + 5, *TILE_0_LAST[4])
            features(1)
            finish_table(1)

            for q in range(QUADS[0], QUADS[0] + 2):
                make_quad(q, q % 2, SLOTS)
            for q in range(QUADS[0], QUADS[0] + 2):
                count_quad(q, q % 2)

            def pair(p, b, slots, at):
                if p == PAIRS - 1:
                    scale_1(4)
                score(at, p, b, slots, pair_pens(p, slots))
                if p == PAIRS - 1:
                    add_1(4)
                weigh(at, p, b, slots, prod)
                if 1 <= p < 4:
                    dense(1, (p - 1,))

            def quad(q, b, at):
                more = not isinstance(q, int) or q < QUADS[1] - 2
                slots = quad_slots(q)
                score(at, q, b, slots, by_tile(quad_pens[b], SLOTS, 4)[:, :, 0:slots], 4)
                if more:
                    make_quad(q + 2, b, quad_slots(q + 2))
                weigh(at, q, b, slots, quad_prod[b], 4)
                if more:
                    count_quad(q + 2, b)
                if isinstance(q, int):
                    if q == QUADS[1] - 3:
                        dve.drain().then_inc(over_ready, 1)
                    if q == QUADS[1] - 1:
                        set_flag(1)
                    if q - 1 in ELU_AT:
                        add_1(ELU_AT[q - 1])
                    if q in ELU_AT:
                        scale_1(ELU_AT[q])

            layer_1(dve, pair, quad, APART)
            scale_1(5)
            add_1(5)
            general(1, whole_residual)


def kernel(**inputs):
    import numpy as np
    import concourse.bacc as bacc
    from concourse.bass_utils import run_bass_kernel_spmd as run

    names = ("x", "adj", "L0_gnn_W", "L0_gnn_a", "L1_gnn_W", "L1_gnn_a")
    nc = bacc.Bacc("TRN2", target_bir_lowering=False, num_devices=1)
    arrays, args = {}, []
    for name in names:
        a = np.ascontiguousarray(inputs[name])
        if name.endswith("_a"):
            a = a.reshape(2 * F, 1)
        arrays[f"in_{name}"] = a
        args.append(nc.dram_tensor(f"in_{name}", a.shape, mybir.dt.from_np(a.dtype), kind="ExternalInput").ap())
    y = nc.dram_tensor("y", (N, F), F32, kind="ExternalOutput").ap()
    build(nc, *args, y)
    r = run(nc, [arrays], core_ids=[0])
    return r.results[0]["y"]
```
